# Optimizing a Trainium2 kernel written in Bass

```python
import numpy as np
import jax
import jax.numpy as jnp

def _softmax(x, axis=-1):
    return jax.nn.softmax(x, axis=axis)

def _gelu(x):
    return jax.nn.gelu(x, approximate=True)

def _silu(x):
    return jax.nn.silu(x)

def _sigmoid(x):
    return jax.nn.sigmoid(x)

def _layernorm(x, axis=-1, eps=1e-05):
    m = jnp.mean(x, axis=axis, keepdims=True)
    v = jnp.var(x, axis=axis, keepdims=True)
    return (x - m) / jnp.sqrt(v + eps)

def _scatter_add(tgt, idx, src, axis=0):
    return tgt.at[idx].add(src)

def _segment_sum(src, seg, n):
    return jax.ops.segment_sum(src, seg, n)
kernel_name = 'mk_cond_seq_d2_seqx_r4_a9ac8d'

def setup_inputs(seed: int=0):
    np.random.seed(seed)
    _w = jnp.asarray

    def _rec_inputs():
        import jax
        import jax.numpy as jnp
        _rk = jax.random.key(seed)
        x = -0.0003482 + 1 * jax.random.normal(jax.random.fold_in(_rk, 1), (32, 256, 288), jnp.float32)
        _lenS = 256 - jax.random.randint(jax.random.fold_in(_rk, 7), (32,), 0, max(1, 256 // 4) + 1, jnp.int32)
        _lenS2 = 256 - jax.random.randint(jax.random.fold_in(_rk, 8), (32,), 0, max(1, 256 // 4) + 1, jnp.int32)
        cond_1152 = 0.00257642 + 1.0011 * jax.random.normal(jax.random.fold_in(_rk, 11), (32, 288), jnp.float32)
        return (x, cond_1152)
    x, cond_1152 = _rec_inputs()

    def _L0_cond_setup():
        import jax, jax.numpy as jnp
        import numpy as np
        H = 288
        NH = 16
        HD = H // NH
        MLP = int(H * 4.0)
        EPS = 1e-06

        def _ln(z, scale=None):
            m = jnp.mean(z, axis=-1, keepdims=True)
            v = jnp.mean(jnp.square(z - m), axis=-1, keepdims=True)
            y = (z - m) * jax.lax.rsqrt(v + EPS)
            if scale is not None:
                y = y * scale
            return y
        key = jax.random.key(seed)
        ks = jax.random.split(key, 16)
        B, N = (16, 256)
        x = jax.random.normal(ks[0], (B, N, H), dtype=jnp.float32)
        c = jax.random.normal(ks[1], (B, H), dtype=jnp.float32)

        def xav(k, fan_in, fan_out):
            lim = np.sqrt(6.0 / (fan_in + fan_out))
            return jax.random.uniform(k, (fan_in, fan_out), jnp.float32, -lim, lim)
        w_mod = 0.02 * jax.random.normal(ks[2], (H, 6 * H), dtype=jnp.float32)
        b_mod = 0.02 * jax.random.normal(ks[3], (6 * H,), dtype=jnp.float32)
        w_qkv = xav(ks[4], H, 3 * H)
        b_qkv = jnp.zeros((3 * H,), jnp.float32)
        g_q = jnp.ones((HD,), jnp.float32)
        g_k = jnp.ones((HD,), jnp.float32)
        w_proj = xav(ks[5], H, H)
        b_proj = jnp.zeros((H,), jnp.float32)
        w1 = xav(ks[6], H, MLP)
        b1 = jnp.zeros((MLP,), jnp.float32)
        w2 = xav(ks[7], MLP, H)
        b2 = jnp.zeros((H,), jnp.float32)
        return dict(x=x, c=c, w_mod=w_mod, b_mod=b_mod, w_qkv=w_qkv, b_qkv=b_qkv, g_q=g_q, g_k=g_k, w_proj=w_proj, b_proj=b_proj, w1=w1, b1=b1, w2=w2, b2=b2)
    _L0_cond_all = _L0_cond_setup()
    _L0_cond_in = {k: v for k, v in _L0_cond_all.items() if k in ('w_mod', 'b_mod', 'w_qkv', 'b_qkv', 'g_q', 'g_k', 'w_proj', 'b_proj', 'w1', 'b1', 'w2', 'b2')}
    del _L0_cond_all

    def _L1_cond_setup():
        import jax, jax.numpy as jnp
        import numpy as np
        B, L, C = (8, 256, 288)
        H = 16
        D = C // H
        FF = int(C * 4.0)
        EPS = 1e-06

        def _layernorm(x):
            mu = jnp.mean(x, axis=-1, keepdims=True)
            var = jnp.mean(jnp.square(x - mu), axis=-1, keepdims=True)
            return (x - mu) * jax.lax.rsqrt(var + EPS)

        def _modulate(x, shift, scale):
            return x * (1.0 + scale) + shift

        def _attention(h, W_qkv, b_qkv, W_proj, b_proj):
            b, l, c = h.shape
            qkv = h @ W_qkv + b_qkv
            qkv = qkv.reshape(b, l, 3, H, D)
            q, k, v = (qkv[:, :, 0], qkv[:, :, 1], qkv[:, :, 2])
            scale = D ** (-0.5)
            scores = jnp.einsum('blhd,bmhd->bhlm', q * scale, k)
            attn = jax.nn.softmax(scores, axis=-1)
            o = jnp.einsum('bhlm,bmhd->blhd', attn, v).reshape(b, l, c)
            return o @ W_proj + b_proj
        key = jax.random.key(seed)
        ks = jax.random.split(key, 12)
        s = 0.02
        return {'x': jax.random.normal(ks[0], (B, L, C), jnp.float32), 'c': jax.random.normal(ks[1], (B, 1, C), jnp.float32), 'W_qkv': jax.random.normal(ks[2], (C, 3 * C), jnp.float32) * s, 'b_qkv': jnp.zeros((3 * C,), jnp.float32), 'W_proj': jax.random.normal(ks[3], (C, C), jnp.float32) * s, 'b_proj': jnp.zeros((C,), jnp.float32), 'W_fc1': jax.random.normal(ks[4], (C, FF), jnp.float32) * s, 'b_fc1': jnp.zeros((FF,), jnp.float32), 'W_fc2': jax.random.normal(ks[5], (FF, C), jnp.float32) * s, 'b_fc2': jnp.zeros((C,), jnp.float32), 'W_ada': jax.random.normal(ks[6], (C, 6 * C), jnp.float32) * s, 'b_ada': jnp.zeros((6 * C,), jnp.float32)}
    _L1_cond_all = _L1_cond_setup()
    _L1_cond_in = {k: v for k, v in _L1_cond_all.items() if k in ('W_qkv', 'b_qkv', 'W_proj', 'b_proj', 'W_fc1', 'b_fc1', 'W_fc2', 'b_fc2', 'W_ada', 'b_ada')}
    del _L1_cond_all
    return {'x': x, 'cond_1152': cond_1152, 'L0_cond_w_mod': _L0_cond_in['w_mod'], 'L0_cond_b_mod': _L0_cond_in['b_mod'], 'L0_cond_w_qkv': _L0_cond_in['w_qkv'], 'L0_cond_b_qkv': _L0_cond_in['b_qkv'], 'L0_cond_g_q': _L0_cond_in['g_q'], 'L0_cond_g_k': _L0_cond_in['g_k'], 'L0_cond_w_proj': _L0_cond_in['w_proj'], 'L0_cond_b_proj': _L0_cond_in['b_proj'], 'L0_cond_w1': _L0_cond_in['w1'], 'L0_cond_b1': _L0_cond_in['b1'], 'L0_cond_w2': _L0_cond_in['w2'], 'L0_cond_b2': _L0_cond_in['b2'], 'L1_cond_W_qkv': _L1_cond_in['W_qkv'], 'L1_cond_b_qkv': _L1_cond_in['b_qkv'], 'L1_cond_W_proj': _L1_cond_in['W_proj'], 'L1_cond_b_proj': _L1_cond_in['b_proj'], 'L1_cond_W_fc1': _L1_cond_in['W_fc1'], 'L1_cond_b_fc1': _L1_cond_in['b_fc1'], 'L1_cond_W_fc2': _L1_cond_in['W_fc2'], 'L1_cond_b_fc2': _L1_cond_in['b_fc2'], 'L1_cond_W_ada': _L1_cond_in['W_ada'], 'L1_cond_b_ada': _L1_cond_in['b_ada']}

def reference(x, cond_1152, L0_cond_w_mod, L0_cond_b_mod, L0_cond_w_qkv, L0_cond_b_qkv, L0_cond_g_q, L0_cond_g_k, L0_cond_w_proj, L0_cond_b_proj, L0_cond_w1, L0_cond_b1, L0_cond_w2, L0_cond_b2, L1_cond_W_qkv, L1_cond_b_qkv, L1_cond_W_proj, L1_cond_b_proj, L1_cond_W_fc1, L1_cond_b_fc1, L1_cond_W_fc2, L1_cond_b_fc2, L1_cond_W_ada, L1_cond_b_ada):
    import jax
    import jax.numpy as jnp

    def _L0_cond_ref(x, c, w_mod, b_mod, w_qkv, b_qkv, g_q, g_k, w_proj, b_proj, w1, b1, w2, b2):
        import jax, jax.numpy as jnp
        import numpy as np
        H = 288
        NH = 16
        HD = H // NH
        MLP = int(H * 4.0)
        EPS = 1e-06

        def _ln(z, scale=None):
            m = jnp.mean(z, axis=-1, keepdims=True)
            v = jnp.mean(jnp.square(z - m), axis=-1, keepdims=True)
            y = (z - m) * jax.lax.rsqrt(v + EPS)
            if scale is not None:
                y = y * scale
            return y
        B, N, _ = x.shape
        mod = jax.nn.swish(c) @ w_mod + b_mod
        sh_msa, sc_msa, g_msa, sh_mlp, sc_mlp, g_mlp = jnp.split(mod, 6, axis=1)
        xn = _ln(x) * (1 + sc_msa[:, None, :]) + sh_msa[:, None, :]
        qkv = xn @ w_qkv + b_qkv
        qkv = qkv.reshape(B, N, 3, NH, HD).transpose(2, 0, 3, 1, 4)
        q, k, v = (qkv[0], qkv[1], qkv[2])
        q = _ln(q, g_q)
        k = _ln(k, g_k)
        attn = jax.nn.softmax(jnp.einsum('bhqd,bhkd->bhqk', q, k) * HD ** (-0.5), axis=-1)
        o = jnp.einsum('bhqk,bhkd->bhqd', attn, v)
        o = o.transpose(0, 2, 1, 3).reshape(B, N, H) @ w_proj + b_proj
        x = x + g_msa[:, None, :] * o
        xn2 = _ln(x) * (1 + sc_mlp[:, None, :]) + sh_mlp[:, None, :]
        h = jax.nn.gelu(xn2 @ w1 + b1, approximate=True)
        x = x + g_mlp[:, None, :] * (h @ w2 + b2)
        return x

    def _L1_cond_ref(x, c, W_qkv, b_qkv, W_proj, b_proj, W_fc1, b_fc1, W_fc2, b_fc2, W_ada, b_ada):
        import jax, jax.numpy as jnp
        import numpy as np
        B, L, C = (8, 256, 288)
        H = 16
        D = C // H
        FF = int(C * 4.0)
        EPS = 1e-06

        def _layernorm(x):
            mu = jnp.mean(x, axis=-1, keepdims=True)
            var = jnp.mean(jnp.square(x - mu), axis=-1, keepdims=True)
            return (x - mu) * jax.lax.rsqrt(var + EPS)

        def _modulate(x, shift, scale):
            return x * (1.0 + scale) + shift

        def _attention(h, W_qkv, b_qkv, W_proj, b_proj):
            b, l, c = h.shape
            qkv = h @ W_qkv + b_qkv
            qkv = qkv.reshape(b, l, 3, H, D)
            q, k, v = (qkv[:, :, 0], qkv[:, :, 1], qkv[:, :, 2])
            scale = D ** (-0.5)
            scores = jnp.einsum('blhd,bmhd->bhlm', q * scale, k)
            attn = jax.nn.softmax(scores, axis=-1)
            o = jnp.einsum('bhlm,bmhd->blhd', attn, v).reshape(b, l, c)
            return o @ W_proj + b_proj
        ada = jax.nn.silu(c) @ W_ada + b_ada
        shift_msa, scale_msa, gate_msa, shift_mlp, scale_mlp, gate_mlp = jnp.split(ada, 6, axis=-1)
        h = _modulate(_layernorm(x), shift_msa, scale_msa)
        x = x + gate_msa * _attention(h, W_qkv, b_qkv, W_proj, b_proj)
        h = _modulate(_layernorm(x), shift_mlp, scale_mlp)
        mlp = jax.nn.gelu(h @ W_fc1 + b_fc1, approximate=True) @ W_fc2 + b_fc2
        x = x + gate_mlp * mlp
        return x
    x = _L0_cond_ref(x, cond_1152, L0_cond_w_mod, L0_cond_b_mod, L0_cond_w_qkv, L0_cond_b_qkv, L0_cond_g_q, L0_cond_g_k, L0_cond_w_proj, L0_cond_b_proj, L0_cond_w1, L0_cond_b1, L0_cond_w2, L0_cond_b2)
    x = _L1_cond_ref(x, cond_1152[:, None, :], L1_cond_W_qkv, L1_cond_b_qkv, L1_cond_W_proj, L1_cond_b_proj, L1_cond_W_fc1, L1_cond_b_fc1, L1_cond_W_fc2, L1_cond_b_fc2, L1_cond_W_ada, L1_cond_b_ada)
    return x

_drawn_inputs = setup_inputs


def setup_inputs(seed=0):
    import zlib

    import numpy as np

    out = dict(_drawn_inputs(seed))
    spreads = {'L0_cond_b_qkv': (0.0, 0.374),
     'L0_cond_g_q': (1.0, 0.6),
     'L0_cond_g_k': (1.0, 0.6),
     'L0_cond_b_proj': (0.0, 0.384),
     'L0_cond_b1': (0.0, 0.51),
     'L0_cond_b2': (0.0, 0.423),
     'L1_cond_b_qkv': (0.0, 0.8),
     'L1_cond_b_proj': (0.0, 0.351),
     'L1_cond_b_fc1': (0.0, 0.8),
     'L1_cond_b_fc2': (0.0, 0.355),
     'L1_cond_b_ada': (0.0, 0.381)}
    factors = {'L0_cond_b_mod': 5.124, 'L1_cond_W_qkv': 8.0, 'L1_cond_W_proj': 5.32}
    for name, (base, spread) in spreads.items():
        noise = np.random.default_rng([zlib.crc32(name.encode()), seed]).standard_normal(out[name].shape)
        drawn = base * np.exp(spread * noise) if base else spread * noise
        out[name] = jnp.asarray(drawn.astype(out[name].dtype))
    for name, factor in factors.items():
        out[name] = (out[name] * factor).astype(out[name].dtype)
    return out
```

```python
from contextlib import ExitStack

import concourse.bass as bass
from concourse import mybir

F32 = mybir.dt.float32
F32R = mybir.dt.float32r
BF16 = mybir.dt.bfloat16
ALU = mybir.AluOpType
ACT = mybir.ActivationFunctionType
AX = mybir.AxisListType

B, N, C = 32, 256, 288
HEADS = 16
HD = C // HEADS
MLP = 4 * C
FC1_LOADS = 3
LAYERS = 2
MLP_WEIGHTS = (("L0_cond_w1", "L0_cond_b1", "L0_cond_w2"), ("L1_cond_W_fc1", "L1_cond_b_fc1", "L1_cond_W_fc2"))
X_LOADS = 8
P = 128
TT = N // P
EPS = 1e-6
SCORE_SCALE = float(HD) ** -0.5
K3 = C // 3

XS_COLS = 2 * C + 32
WIDE_ROWS = [128, 128, 128, 128, 98]
WIDE_CHUNKS = 7
WIDE_PAIRS = [(0, 0), (1, 1), (2, 2), (3, 3), (4, 4), (5, 0), (6, 1)]

QK = 2 * C
QK_M = 7 * HD
QK_CHUNKS = [(m, min(QK_M, QK - m)) for m in range(0, QK, QK_M)]
STACK = 6 * HD
VW = HD + 2
PV_HEADS = 4
GROUPS = HEADS // PV_HEADS

STACK_RING, V_RING, P_RING, PSUM_RING = 3, 5, 6, 3
Z_RING, PARTS_RING = 4, 4

MAX_LEAD = HEADS + 8
FRONT_START = -72
CHUNK_SLOTS = [-57, -56, -54, -53, -52]
VALUE_SLOTS = [-50, -49]
STACKS_SLOT = -32
PROJ_SLOTS = [(32, 34), (36, 37)]


class Engine:

    def __init__(self, sem):
        self.sem, self.count, self.queue, self.seen = sem, 0, [], {}

    def wait(self, *after):
        for mark in flat(after):
            sem, value = mark
            if self.seen.get(id(sem), 0) < value:
                self.seen[id(sem)] = value
                self.queue.append(lambda e, s=sem, v=value: e.wait_ge(s, v))

    def do(self, emit, *after):
        self.wait(*after)
        self.count += 1
        self.queue.append(lambda e, f=emit: f(e).then_inc(self.sem, 1))
        return (self.sem, self.count)

    def dma(self, out, in_, stream, *after):
        self.wait(*after)
        stream.count += 16
        self.queue.append(lambda e, s=stream.sem: e.dma_start(out, in_).then_inc(s, 16))
        return (stream.sem, stream.count)

    def play(self, e):
        for step in self.queue:
            step(e)


class Stream:

    def __init__(self, sem):
        self.sem, self.count = sem, 0


def flat(marks):
    for m in marks:
        if m is None:
            continue
        if isinstance(m, list):
            yield from flat(m)
        else:
            yield m


class Bank:

    def __init__(self, ap):
        self.ap, self.free = ap, None


class Banks:

    def __init__(self, banks):
        self.idle = list(banks)

    def take(self):
        return self.idle.pop(0)

    def put(self, bank, mark):
        bank.free = mark
        self.idle.append(bank)
        return mark


class Agenda:

    def __init__(self, slot):
        self.slot, self.started, self.waiting = slot, 0, []

    def start(self, g, last=False):
        self.started += 1
        self.step((last, self.started), g)

    def step(self, age, g):
        for then in g:
            if isinstance(then, int):
                if then > self.slot:
                    self.waiting.append((age, then, g))
                    return
            else:
                self.start(then)

    def run(self, slot):
        self.slot = slot
        due = sorted((w for w in self.waiting if w[1] <= slot), key=lambda w: w[0])
        self.waiting = [w for w in self.waiting if w[1] > slot]
        for age, _, g in due:
            self.step(age, g)


def build(nc, a, out):
    outer = ExitStack()
    with outer:
        def sem(name):
            return outer.enter_context(nc.semaphore(name))

        def stream(name):
            return Stream(sem(name))

        pe, act, dve, pool, sp = (Engine(sem(n)) for n in ("pe_done", "act_done", "dve_done", "pool_done", "sp_unused"))
        engines = [pe, act, dve, pool, sp]

        def sb_in(scope, name, shape, dt=F32):
            return scope.enter_context(nc.sbuf_tensor(name, shape, dt))

        def phase(name, build_phase):
            with ExitStack() as scope:
                build_phase(lambda n, shape, dt=F32: sb_in(scope, f"{name}_{n}", shape, dt))
                marks = [(e.sem, e.count) for e in engines if e.count]
                marks += [(s.sem, s.count) for s in streams if s.count]
                for e in engines:
                    e.wait(marks)

        streams = []

        def new_stream(name):
            s = stream(name)
            streams.append(s)
            return s

        x_sb = sb_in(outer, "x_resident", [P, B * TT, C])
        ident_wide = sb_in(outer, "identity_between_zeros", [P, 3 * P], F32R)
        ident = ident_wide[:, P:2 * P].bitcast(F32)
        head_ones = sb_in(outer, "head_block_ones", [P, P])
        minus_half = sb_in(outer, "minus_half", [P, TT])
        minus_lo_row = sb_in(outer, "minus_one_on_low_rows", [P, 1])
        eps_col = sb_in(outer, "eps_column", [P, 1])
        qk_gain = sb_in(outer, "qk_gain", [P, len(QK_CHUNKS)])
        w_attn = sb_in(outer, "w_qkv_stacked", [P, WIDE_CHUNKS, 3 * C], F32R)
        w_proj = sb_in(outer, "w_proj_by_heads", [P, GROUPS, C])
        psum = [Bank(outer.enter_context(nc.psum_tensor(f"psum{i}", [P, 512], F32))) for i in range(8)]

        def scratch(name, shape, dt=F32):
            return nc.dram_tensor(name, shape, dt).ap()

        mod_d = scratch("modulation", (LAYERS, B, 7 * C))
        group = MLP // FC1_LOADS
        qkv_d = scratch("qkv_stacked", (P, WIDE_CHUNKS, 3 * C))
        fc1_d = [[scratch(f"fc1_stacked_{l}_{g}", (P, WIDE_CHUNKS, group)) for g in range(FC1_LOADS)] for l in range(LAYERS)]
        fc2_d = [scratch(f"fc2_by_rows_{l}", (P, MLP // P, C)) for l in range(LAYERS)]
        parts_d = [scratch(f"qk_parts_{i}", (3, QK, N), BF16) for i in range(2)]
        recip_d = scratch("row_reciprocals", (PV_HEADS, GROUPS * N))

        s_x = [stream(f"x_loaded_{i}") for i in range(X_LOADS)]
        s_out = new_stream("out_stored")
        s_cond = new_stream("cond_loaded")
        s_w_mod = [new_stream(f"w_mod_loaded_{l}") for l in range(LAYERS)]
        s_mod_rows = [new_stream(f"mod_rows_stored_{l}") for l in range(LAYERS)]
        s_w = new_stream("attn_weights_loaded")
        s_w_proj = new_stream("proj_weights_loaded")
        s_w_fc1 = [new_stream(f"fc1_weights_loaded_{i}") for i in range(FC1_LOADS)]
        s_w_fc2 = new_stream("fc2_weights_loaded")
        s_order_fc1 = [stream(f"fc1_arranged_{l}") for l in range(LAYERS)]
        s_order_fc2 = [stream(f"fc2_arranged_{l}") for l in range(LAYERS)]
        s_order_qkv = stream("qkv_arranged")
        s_mod = new_stream("attn_mod_loaded")
        s_gate = new_stream("attn_gate_loaded")
        s_mod2 = [new_stream(f"mlp_mod_loaded_{i}") for i in range(2)]
        s_gate2 = [new_stream(f"mlp_gate_loaded_{i}") for i in range(2)]
        s_parts = [new_stream(f"parts_stored_{m}") for m in range(len(QK_CHUNKS))]
        s_stack = [new_stream(f"stack_loaded_{i}") for i in range(STACK_RING)]
        s_max = new_stream("maxima_placed")
        s_sums = new_stream("sums_spread")
        s_recip = new_stream("reciprocals_stored")
        s_recip_in = new_stream("reciprocals_loaded")

        def copy(e, out_, in_, *after):
            if e is act:
                return e.do(lambda q: q.activation(out_, in_, ACT.Copy), *after)
            return e.do(lambda q: q.tensor_copy(out_, in_), *after)

        def tt(e, out_, in0, in1, op, *after):
            return e.do(lambda q: q.tensor_tensor(out_, in0, in1, op), *after)

        def stt(out_, in0, scalar, in1, op0, op1, *after):
            return dve.do(lambda q: q.scalar_tensor_tensor(out=out_, in0=in0, scalar=scalar, in1=in1, op0=op0, op1=op1), *after)

        def func(out_, in_, f, *after, **kw):
            return act.do(lambda q: q.activation(out_, in_, f, **kw), *after)

        def matmuls(steps, *after):
            def emit(q):
                last = None
                for i, (o, l, r) in enumerate(steps):
                    last = q.matmul(o, l, r, start=(i == 0), stop=(i == len(steps) - 1))
                return last
            return pe.do(emit, *after)

        def fp(ap):
            return ap.bitcast(F32)

        def wide_steps(out_, weights, acts, w_cols, a_cols, weights_stationary):
            steps = []
            for kw, ka in WIDE_PAIRS:
                rows = WIDE_ROWS[ka]
                w = weights[0:rows, kw, w_cols[0]:w_cols[1]]
                x = acts[0:rows, ka, a_cols[0]:a_cols[1]]
                steps.append((out_, w, x) if weights_stationary else (out_, x, w))
            return steps

        draft = w_proj[:].rearrange("p g n -> p (g n)")[:, 0:3 * P]
        k = dve.do(lambda q: q.memset(draft, 0.0))
        k = pool.do(lambda q: q.affine_select(out=draft, in_=draft, compare_op=ALU.not_equal, fill=1.0,
                                              base=P, pattern=[[-1, 3 * P]], channel_multiplier=1), k)
        ident_ok = copy(dve, ident_wide[:], draft, k)
        k = dve.do(lambda q: q.memset(head_ones[:], 1.0))
        blocks = head_ones[:, 0:QK_M].rearrange("p (j d) -> p j d", d=HD)
        k = pool.do(lambda q: q.affine_select(out=blocks, in_=blocks, compare_op=ALU.is_ge, fill=0.0,
                                              base=0, pattern=[[-HD, 7], [0, HD]], channel_multiplier=1), k)
        head_ones_ok = pool.do(lambda q: q.affine_select(out=blocks, in_=blocks, compare_op=ALU.is_ge, fill=0.0,
                                                         base=HD - 1, pattern=[[HD, 7], [0, HD]], channel_multiplier=-1), k)
        dve.do(lambda q: q.memset(eps_col[:], EPS))
        k = dve.do(lambda q: q.memset(minus_lo_row[:], -1.0))
        k = dve.do(lambda q: q.memset(minus_lo_row[0:64, :], 0.0), k)
        dve.do(lambda q: q.memset(minus_lo_row[96:97, :], 0.0), k)
        dve.do(lambda q: q.memset(minus_half[:], -0.5))
        const_ok = (dve.sem, dve.count)

        gk_col = sb_in(outer, "g_k_columns", [P, len(QK_CHUNKS)])
        dve.do(lambda q: q.memset(qk_gain[:], 1.0))
        const_gain = dve.do(lambda q: q.memset(gk_col[:], 1.0))

        prepared, x_marks = {}, {}

        def prepare(sb):
            cond = sb("cond", [B, C])
            silu_a = sb("silu_denominator", [B, C])
            silu_b = sb("silu", [B, C])
            silu_t = sb("silu_transposed", [K3, 3, B])
            loaded = sp.dma(cond[:], a["cond_1152"], s_cond)
            k = func(silu_a[:], cond[:], ACT.Exp, loaded, scale=-1.0)
            k = dve.do(lambda q: q.tensor_scalar(silu_a[:], silu_a[:], 1.0, None, ALU.add), k)
            k = dve.do(lambda q: q.reciprocal(silu_a[:], silu_a[:]), k)
            silu_ok = tt(dve, silu_b[:], cond[:], silu_a[:], ALU.mult, k)
            for i in range(3):
                t = pe.do(lambda q, i=i: q.transpose(psum[i].ap[0:K3, 0:B], silu_b[:, K3 * i:K3 * i + K3], ident[0:B, 0:B]),
                          silu_ok, ident_ok)
                silu_t_ok = psum[i].free = copy(dve, silu_t[:, i, :], psum[i].ap[0:K3, 0:B], t)
            w_mod = [sb(f"w_mod{l}", [K3, 3, 6 * C]) for l in range(LAYERS)]
            b_mod = [sb(f"b_mod{l}", [B, 6 * C]) for l in range(LAYERS)]
            b_2 = [sb(f"b_fc2_{l}", [B, C]) for l in range(LAYERS)]
            rows = [sb(f"mod_rows{l}", [B, 7 * C]) for l in range(LAYERS)]
            order = [1, 0, 2, 4, 3, 5]
            names = (("L0_cond_w_mod", "L0_cond_b_mod", "L0_cond_b2"), ("L1_cond_W_ada", "L1_cond_b_ada", "L1_cond_b_fc2"))

            def load_modulation(l):
                w, bias, b2 = names[l]
                sp.dma(w_mod[l][:], a[w].rearrange("(i p) n -> p i n", p=K3), s_w_mod[l])
                sp.dma(b_mod[l][:], a[bias].rearrange("(o n) -> o n", o=1).broadcast_to([B, 6 * C]), s_w_mod[l])
                return sp.dma(b_2[l][:], a[b2].rearrange("(o n) -> o n", o=1).broadcast_to([B, C]), s_w_mod[l])

            def modulation(l, loaded):
                done = []
                for j in range(6):
                    bank = psum[3 + j % 3]
                    mm = matmuls([(bank.ap[0:B, 0:C], silu_t[:, i, :], w_mod[l][:, i, C * j:C * j + C]) for i in range(3)],
                                 loaded, silu_t_ok, bank.free)
                    to = order.index(j)
                    r = bank.free = stt(rows[l][:, C * to:C * to + C], bank.ap[0:B, 0:C], 1.0 if j in (1, 4) else 0.0,
                                        b_mod[l][:, C * j:C * j + C], ALU.add, ALU.add, mm, loaded)
                    done.append(r)
                g = tt(dve, rows[l][:, 6 * C:7 * C], rows[l][:, 5 * C:6 * C], b_2[l][:], ALU.mult, done)
                prepared["mod", l] = sp.dma(mod_d[l], rows[l][:], s_mod_rows[l], g)

            mod_loaded = load_modulation(0)
            def load_x(g, *after):
                n = B // X_LOADS
                mark = act.dma(x_sb[:, TT * n * g:TT * n * (g + 1), :],
                               a["x"][n * g:n * (g + 1)].rearrange("b (t p) c -> p (b t) c", p=P), s_x[g], *after)
                for i in range(TT * n * g, TT * n * (g + 1)):
                    x_marks[i] = mark
            load_x(0)
            raw = sb("raw_qkv", [P, WIDE_CHUNKS, 3 * C])
            raw_ok = arrange_stacked(sp, raw, "L0_cond_w_qkv", "L0_cond_b_qkv", slice(0, 3 * C), s_w)
            mod_1_loaded = load_modulation(1)
            modulation(0, mod_loaded)

            mean = sb("head_means", [P, 2 * HEADS])
            centred = []
            for c in range(WIDE_CHUNKS):
                n = WIDE_ROWS[c] if c < len(WIDE_ROWS) else P
                m = mean[0:n, :]
                qk = raw[0:n, c, 0:QK].rearrange("p (h d) -> p h d", d=HD)
                k = dve.do(lambda q, m=m, qk=qk: q.tensor_reduce(m, qk, AX.X, ALU.add), raw_ok, centred[-1:])
                k = dve.do(lambda q, m=m: q.tensor_scalar(m, m, -1.0 / HD, None, ALU.mult), k)
                mb = m.rearrange("p (h o) -> p h o", o=1).broadcast_to([n, 2 * HEADS, HD])
                centred.append(tt(dve, qk, qk, mb, ALU.add, k))
            split_ok = split_stacked(raw, w_attn, slice(0, 3 * C), proj_space, centred + [raw_ok])
            prepared["attn_weights", 0] = split_ok + load_proj(0, split_ok)
            modulation(1, mod_1_loaded)
            for g in range(1, X_LOADS // 2):
                load_x(g, mod_1_loaded)
            for l in range(LAYERS):
                w1, b1, w2 = MLP_WEIGHTS[l]
                for g in range(FC1_LOADS):
                    prepared["fc1", l] = arrange_stacked(act, fc1_d[l][g], w1, b1, slice(group * g, group * (g + 1)), s_order_fc1[l])
                prepared["fc2", l] = act.dma(fc2_d[l], a[w2].rearrange("(c p) n -> p c n", p=P), s_order_fc2[l])
                if l == 0:
                    for g in range(X_LOADS // 2, X_LOADS):
                        load_x(g)
                    prepared["qkv", 1] = arrange_stacked(act, qkv_d, "L1_cond_W_qkv", "L1_cond_b_qkv", slice(0, 3 * C), s_order_qkv)

        proj_space = w_proj[:].rearrange("p g n -> p (g n)").bitcast(F32R)

        def arrange_stacked(queue, dst, w, bias, cols, st, *after):
            w, bias = a[w][:, cols], a[bias].rearrange("(o n) -> o n", o=1)[:, cols]
            moves = [
                (dst[:, 0:2, :], w[0:256, :].rearrange("(i p) n -> p i n", p=P)),
                (dst[0:32, 2, :], w[256:288, :]), (dst[32:128, 2, :], w[0:96, :]),
                (dst[:, 3, :], w[96:224, :]),
                (dst[0:64, 4, :], w[224:288, :]), (dst[64:96, 4, :], w[256:288, :]),
                (dst[96:98, 4, :], bias.broadcast_to([2, cols.stop - cols.start])),
                (dst[:, 5:7, :], w[0:256, :].rearrange("(i p) n -> p i n", p=P)),
            ]
            for d, s in moves:
                mark = queue.dma(d, s, st, *after)
            return mark

        def load_stacked(dst, src, cols, st, *after):
            rows = WIDE_ROWS[4]
            sp.dma(fp(dst[:, 0:4, cols]), src[:, 0:4, :], st, *after)
            sp.dma(fp(dst[0:rows, 4, cols]), src[0:rows, 4, :], st, *after)
            return sp.dma(fp(dst[:, 5:7, cols]), src[:, 5:7, :], st, *after)

        def split_stacked(src, dst, cols, tmp, *loaded):
            rows = WIDE_ROWS[4]
            mixed, low = dst[0:rows, 4, cols], dst[:, 5:7, cols]
            t = tmp[0:rows, 0:cols.stop - cols.start]
            hk = copy(act, dst[:, 0:4, cols], fp(src[:, 0:4, cols]), *loaded)
            tk = copy(act, t, fp(src[0:rows, 4, cols]), *loaded)
            lk = tt(dve, low, fp(src[:, 5:7, cols]), fp(dst[:, 0:2, cols]), ALU.subtract, hk, *loaded)
            mk = stt(mixed, fp(t), minus_lo_row[0:rows, :], fp(src[0:rows, 4, cols]), ALU.mult, ALU.add, tk, const_ok, *loaded)
            return [hk, tk, lk, mk]

        def load_proj(l, *after):
            zero = dve.do(lambda q: q.memset(w_proj[:], 0.0), *after)
            wp, bp = (("L0_cond_w_proj", "L0_cond_b_proj"), ("L1_cond_W_proj", "L1_cond_b_proj"))[l]
            by_head = a[wp].rearrange("(g i d) n -> i d g n", i=PV_HEADS, d=HD)
            for i in range(PV_HEADS):
                sp.dma(w_proj[32 * i:32 * i + HD, :, :], by_head[i], s_w_proj, zero)
            mark = sp.dma(w_proj[HD:HD + 1, 0, :], a[bp].rearrange("(o n) -> o n", o=1), s_w_proj, zero)
            if l == 0:
                for m, (c0, rows) in enumerate(QK_CHUNKS):
                    n = min(rows, C - c0) // HD
                    if n > 0:
                        for dst, g in ((qk_gain, "L0_cond_g_q"), (gk_col, "L0_cond_g_k")):
                            mark = sp.dma(dst[0:n * HD, m:m + 1], a[g].rearrange("(o d) -> o d", o=1).broadcast_to([n, HD]),
                                          s_w_proj, const_gain)
                return [mark, tt(dve, qk_gain[:], qk_gain[:], gk_col[:], ALU.mult, mark)]
            return [mark]

        class Normaliser:

            def __init__(self, sb, ring):
                self.stats = sb("ln_stats", [P, TT, 6])
                self.mv = sb("ln_mean_var", [P, TT, 2])
                self.rstd = sb("ln_rstd", [P, TT])
                self.scaled = sb("ln_scaled", [P, C])
                self.y = [sb(f"ln_modulated{i}", [P, C]) for i in range(2)]
                self.xs = [sb(f"ln_split{i}", [P, XS_COLS], F32R) for i in range(TT)]
                self.xt = [sb(f"ln_transposed{i}", [P, len(WIDE_ROWS), N], F32R) for i in range(ring)]
                self.xt_free = [None] * ring
                self.xs_free = [None] * TT
                self.stats_free = self.mv_free = self.rstd_free = self.scaled_free = None
                self.y_free = [None, None]
                self.ones_ok = [dve.do(lambda q, t=t: q.memset(fp(t[96:98, 4, :]), 1.0)) for t in self.xt]

            def run(self, b, start, scale_row, shift_row, mod_ok, take, put):
                hi_cols, lo_cols, dup = slice(0, C), slice(C, 2 * C), slice(2 * C, XS_COLS)
                ring = b % len(self.xt)
                agg = []
                for t in range(TT):
                    xt = x_sb[:, TT * b + t, :]
                    st = dve.do(lambda q, t=t, xt=xt: q.bn_stats(self.stats[:, t, :], xt), x_marks[TT * b + t], self.stats_free)
                    agg.append(dve.do(lambda q, t=t: q.bn_aggr(self.mv[:, t, :], self.stats[:, t, :]), st, self.mv_free))
                self.stats_free = agg
                yield start + 1
                k = pool.do(lambda q: q.tensor_scalar(self.rstd[:], self.mv[:, :, 1], EPS, None, ALU.add), agg, self.rstd_free)
                rstd_ok = tt(pool, self.rstd[:], self.rstd[:], minus_half[:, 0:TT], ALU.pow, k, const_ok)
                yield start + 3
                done = []

                def modulate(t):
                    u = stt(self.scaled[:], x_sb[:, TT * b + t, :], self.mv[:, t, 0:1], scale_row, ALU.subtract, ALU.mult,
                            agg, mod_ok, self.scaled_free)
                    y = self.scaled_free = stt(self.y[t][:], self.scaled[:], self.rstd[:, t:t + 1], shift_row, ALU.mult, ALU.add,
                                               u, rstd_ok, self.y_free[t])
                    return y

                def high(t, y):
                    return copy(act, self.xs[t][:, hi_cols], self.y[t][:], y, self.xs_free[t])

                def low(t, h):
                    xs = self.xs[t]
                    lo = tt(pool, xs[:, lo_cols], self.y[t][:], fp(xs[:, hi_cols]), ALU.subtract, h, self.xs_free[t])
                    self.y_free[t] = [h, lo]
                    d = copy(pool, xs[:, dup], fp(xs[:, 256:C]), h, self.xs_free[t])
                    done.append([h, lo, d])

                y0 = modulate(0)
                yield start + 4
                y1 = modulate(1)
                self.mv_free = self.rstd_free = self.mod_read = y1
                h0 = high(0, y0)
                yield start + 5
                h1 = high(1, y1)
                low(0, h0)
                yield start + 6
                low(1, h1)
                yield start + 8
                evac = []
                pending = None
                for n, pair in enumerate(((0, 1), (2, 3), (4,), None)):
                    if pending:
                        tr, bank, rows, c0, n_c = pending
                        evac.append(copy(act, self.xt[ring][0:rows, c0:c0 + n_c, :],
                                         bank.ap[0:rows, 0:n_c * N].rearrange("p (c n) -> p c n", c=n_c), tr,
                                         self.xt_free[ring], self.ones_ok[ring]))
                        put(bank, evac[-1])
                    if pair is None:
                        break
                    bank = take()
                    rows = 96 if pair == (4,) else P

                    def emit(q, pair=pair, bank=bank, rows=rows):
                        for j, c in enumerate(pair):
                            for t in range(TT):
                                last = q.matmul(bank.ap[0:rows, j * N:j * N + N], self.xs[t][:, c * P:c * P + rows],
                                                ident_wide[:, P - t * P:P - t * P + N], start=(t == 0), stop=(t == TT - 1))
                        return last
                    tr = pe.do(emit, done, bank.free, ident_ok)
                    pending = (tr, bank, rows, pair[0], len(pair))
                    self.xs_free = [tr] * TT
                    yield start + 9 + n
                self.ready = (self.xt[ring], evac)


        def attention(l):
            def run(sb):
                banks = Banks(psum[8 - PSUM_RING:])
                take, put = banks.take, banks.put

                ln = Normaliser(sb, 1)
                mod = sb("scale_shift", [P, 2 * C])
                gate = sb("gate", [P, C])
                parts = [sb(f"qk_parts{i}", [P, 3, N], BF16) for i in range(PARTS_RING)]
                rest = [sb(f"qk_rest{i}", [P, N]) for i in range(2)]
                if l == 0:
                    z_sb = [sb(f"qk_centred{i}", [P, N]) for i in range(Z_RING)]
                    sq_sb = [sb(f"qk_squares{i}", [P, N]) for i in range(2)]
                    rstd_sb = [sb(f"qk_rstd{i}", [P, N]) for i in range(2)]
                q_st = [sb(f"q_stack{i}", [P, HEADS, N], BF16) for i in range(STACK_RING)]
                k_st = [sb(f"k_stack{i}", [P, HEADS, N], BF16) for i in range(STACK_RING)]
                v_sb = [sb(f"v{i}", [P, TT, HEADS, VW]) for i in range(V_RING)]
                probs = [sb(f"probs{i}", [P, TT * N]) for i in range(P_RING)]
                o_t = [sb(f"o_transposed{i}", [P, GROUPS * N]) for i in range(2)]
                recip_b = sb("reciprocals", [P, GROUPS * N])
                sums = sb("row_sums", [P, PV_HEADS * GROUPS * N // P])
                recip = sb("row_reciprocals", [P, PV_HEADS * GROUPS * N // P])
                maxes = [sb(f"maxima{i}", [P, HEADS, TT]) for i in range(2)]
                neg_hi = sb("neg_max_hi", [HEADS * TT, P], BF16)
                neg_lo = sb("neg_max_lo", [HEADS * TT, P], BF16)
                gated = sb("gated", [P, C])

                w_ok = prepared["attn_weights", l]
                k_ones = [dve.do(lambda q, t=t: q.memset(t[96:128, :, :], 1.0)) for t in k_st]
                v_one = []
                for t in v_sb:
                    dve.do(lambda q, t=t: q.memset(t[:, :, :, HD:HD + 1], 1.0))
                    v_one.append(dve.do(lambda q, t=t: q.memset(t[:, :, :, HD + 1:VW], 0.0)))
                pv = psum[4]
                pv.free = dve.do(lambda q: q.memset(pv.ap[:, 0:N], 0.0))

                if l == 0:
                    act.queue.append(lambda q: q.preload_act_table_set("natural_log_exp_and_others"))
                live = []
                parts_free = [None] * PARTS_RING
                rest_free, z_free = [None, None], [None] * Z_RING
                part_marks = {}
                stack_ok, v_ok = {}, {}
                scratch_free = [None, None]
                last_scores = {}
                max_ok, max_t_ok, exp_ok, pv_done, neg_ok = {}, {}, {}, {}, {}
                smax_free, st_free = [None, None], [None, None]
                probs_free = [None] * P_RING
                sq_free, rstd_free = [None, None], [None, None]
                state = {"mod_free": None, "gate_free": None, "neg": None,
                         "sums": None, "recip": None, "recip_b": None, "gated": None}
                o_free = [None, None]
                v_free = [None] * V_RING

                def load_mod(b):
                    return sp.dma(mod[:], mod_d[l, b:b + 1, 0:2 * C].broadcast_to([P, 2 * C]), s_mod, state["mod_free"],
                                  prepared["mod", l])

                chunks_done = [0]

                def qk_chunk(b, m, xt, xt_ok):
                    c0, rows = QK_CHUNKS[m]
                    slot = HEADS * b + CHUNK_SLOTS[m]
                    bank = take()
                    mm = matmuls(wide_steps(bank.ap[0:rows, 0:N], w_attn, xt, (c0, c0 + rows), (0, N), True),
                                 xt_ok, w_ok, bank.free)
                    n = chunks_done[0]
                    chunks_done[0] += 1
                    i, pi, zi = n % 2, n % PARTS_RING, n % Z_RING
                    a_part, b_part, c_part = (parts[pi][0:rows, j, :] for j in range(3))
                    r = rest[i][0:rows, :]
                    yield slot + 1
                    if l == 1:
                        ak = copy(act, a_part, bank.ap[0:rows, 0:N], mm, parts_free[pi])
                        yield slot + 2
                        rk = put(bank, tt(dve, r, bank.ap[0:rows, 0:N], a_part, ALU.subtract, ak, rest_free[i]))
                        yield slot + 3
                        bk = copy(act, b_part, r, rk, parts_free[pi])
                        yield slot + 4
                    else:
                        z, sq, qk_rstd = z_sb[zi][0:rows, :], sq_sb[i][0:rows, :], rstd_sb[i][0:rows, :]
                        zk = put(bank, copy(act, z, bank.ap[0:rows, 0:N], mm, z_free[zi]))
                        sk = func(sq, z, ACT.Square, zk, sq_free[i])
                        yield slot + 2
                        bank = take()
                        vk = sq_free[i] = pe.do(lambda q: q.matmul(bank.ap[0:rows, 0:N], head_ones[0:rows, 0:rows],
                                                                   sq, start=True, stop=True),
                                                sk, bank.free, head_ones_ok)
                        yield slot + 3
                        lk = put(bank, func(qk_rstd, bank.ap[0:rows, 0:N], ACT.Ln, vk, rstd_free[i], const_ok,
                                            bias=eps_col[0:rows, :], scale=1.0 / HD))
                        ek = func(qk_rstd, qk_rstd, ACT.Exp, lk, scale=-0.5)
                        yield slot + 4
                        yk = rstd_free[i] = stt(z, z, qk_gain[0:rows, m:m + 1], qk_rstd, ALU.mult, ALU.mult, ek, zk)
                        yield slot + 5
                        ak = copy(act, a_part, z, yk, parts_free[pi])
                        yield slot + 6
                        rk = z_free[zi] = tt(dve, r, z, a_part, ALU.subtract, ak, rest_free[i])
                        bk = copy(dve, b_part, r, rk, parts_free[pi])
                        yield slot + 7
                    ck = rest_free[i] = tt(pool, c_part, r, b_part, ALU.subtract, bk)
                    dst = parts_d[b % 2][:, c0:c0 + rows, :].rearrange("j r n -> r j n")
                    part_marks[b, m] = parts_free[pi] = sp.dma(dst, parts[pi][0:rows, :, :], s_parts[m], ck, scratch_free[b % 2])

                def load_stacks(b):
                    ring, d = b % STACK_RING, parts_d[b % 2]
                    after = [part_marks[b, m] for m in range(len(QK_CHUNKS))] + [last_scores.get(b - STACK_RING), k_ones]
                    for j, (qp, kp) in enumerate(((0, 0), (0, 1), (0, 2), (1, 0), (1, 1), (2, 0))):
                        for st, p, c0 in ((q_st, qp, 0), (k_st, kp, C)):
                            mark = sp.dma(st[ring][HD * j:HD * j + HD, :, :],
                                          d[p, c0:c0 + C, :].rearrange("(h r) n -> r h n", r=HD), s_stack[ring], after)
                    stack_ok[b] = scratch_free[b % 2] = mark


                def value_tile(b, t, xt, xt_ok):
                    bank = take()
                    mm = matmuls(wide_steps(bank.ap[:, 0:C], w_attn, xt, (QK, 3 * C), (t * P, t * P + P), False),
                                 xt_ok, w_ok, bank.free)
                    ln.xt_free = [mm]
                    yield HEADS * b + VALUE_SLOTS[t] + 1
                    vk = copy(dve, v_sb[b % V_RING][:, t, :, 0:HD], bank.ap[:, 0:C].rearrange("p (h d) -> p h d", d=HD),
                              mm, v_free[b % V_RING], v_one)
                    v_ok.setdefault(b, []).append(put(bank, vk))

                def front(b):
                    mod_ok = load_mod(b)
                    start = HEADS * b + FRONT_START
                    yield start + 3
                    yield from ln.run(b, start + 3, mod[:, 0:C], mod[:, C:2 * C], mod_ok, take, put)
                    state["mod_free"] = ln.mod_read
                    xt, xt_ok = ln.ready
                    for m, slot in enumerate(CHUNK_SLOTS):
                        yield HEADS * b + slot
                        yield qk_chunk(b, m, xt, xt_ok)
                    for t, slot in enumerate(VALUE_SLOTS):
                        yield HEADS * b + slot
                        yield value_tile(b, t, xt, xt_ok)
                    yield HEADS * b + STACKS_SLOT
                    load_stacks(b)

                def place_maxima(b):
                    slot = HEADS * b - MAX_LEAD + HEADS + 1
                    yield slot + 1
                    bank = take()
                    rows = HEADS * TT
                    tr = max_t_ok[b] = pe.do(
                        lambda q: q.transpose(bank.ap[0:rows, 0:P], maxes[b % 2][:].rearrange("p h t -> p (h t)"), ident),
                        max_ok[b, HEADS - 1], bank.free, ident_ok)
                    yield slot + 2
                    hk = dve.do(lambda q: q.tensor_scalar(neg_hi[:], bank.ap[0:rows, 0:P], -1.0, None, ALU.mult), tr, state["neg"])
                    lk = put(bank, stt(neg_lo[:], bank.ap[0:rows, 0:P], -1.0, neg_hi[:], ALU.mult, ALU.subtract, hk))
                    yield slot + 3
                    for src, row in ((neg_hi, STACK), (neg_lo, STACK + 1)):
                        dst = q_st[b % STACK_RING][row:row + 1, :, :].rearrange("o h (t n) -> o (h t) n", t=TT)
                        neg_ok[b] = state["neg"] = sp.dma(dst, src[:], s_max, lk, last_scores.get(b - STACK_RING))

                def max_scores(b, h):
                    ring, i = b % STACK_RING, h % 2
                    bank = psum[i]
                    qs, ks = q_st[ring], k_st[ring]

                    def emit(q):
                        for t in range(TT):
                            last = q.matmul(bank.ap[:, t * N:t * N + N], qs[0:STACK, h, t * P:t * P + P], ks[0:STACK, h, :],
                                            start=True, stop=True)
                        return last
                    return pe.do(emit, stack_ok[b], smax_free[i])

                def reduce_max(b, h, mm):
                    i = h % 2
                    max_ok[b, h] = smax_free[i] = dve.do(
                        lambda q: q.tensor_reduce(maxes[b % 2][:, h, :], psum[i].ap[:].rearrange("p (t n) -> p t n", t=TT), AX.X, ALU.max),
                        mm, max_t_ok.get(b - 2))

                def shifted_scores(b, h):
                    ring, i = b % STACK_RING, h % 2
                    bank = psum[2 + i]
                    qs, ks = q_st[ring], k_st[ring]

                    def emit(q):
                        for t in range(TT):
                            last = q.matmul(bank.ap[:, t * N:t * N + N], ks[0:STACK + 2, h, t * P:t * P + P],
                                            qs[0:STACK + 2, h, :], start=True, stop=True)
                        return last
                    mm = pe.do(emit, stack_ok[b], neg_ok[b], st_free[i])
                    last_scores[b] = mm
                    return mm

                def exponentials(b, h, mm):
                    i = h % 2
                    r = (b * HEADS + h) % P_RING
                    exp_ok[b, h] = st_free[i] = func(probs[r][:], psum[2 + i].ap[:], ACT.Exp, mm, probs_free[r], scale=SCORE_SCALE)

                def weigh_values(b, g):
                    def emit(q):
                        for t in range(TT):
                            for i in range(PV_HEADS):
                                h = g * PV_HEADS + i
                                r = (b * HEADS + h) % P_RING
                                last = q.matmul(pv.ap[32 * i:32 * i + VW, 0:N], v_sb[b % V_RING][:, t, h, :],
                                                probs[r][:, t * N:t * N + N], start=(t == 0), stop=(t == TT - 1))
                        return last
                    mm = pe.do(emit, v_ok[b], [exp_ok[b, g * PV_HEADS + i] for i in range(PV_HEADS)], pv.free)
                    for i in range(PV_HEADS):
                        probs_free[(b * HEADS + g * PV_HEADS + i) % P_RING] = mm
                    v_free[b % V_RING] = mm
                    return mm

                def values(b, g, slot):
                    mm = weigh_values(b, g)
                    yield slot + 1
                    pv_done[b, g] = pv.free = copy(act, o_t[b % 2][:, g * N:g * N + N], pv.ap[:, 0:N], mm, o_free[b % 2])

                    if g == GROUPS - 1:
                        yield back(b)

                def back(b):
                    first = HEADS * b + HEADS + 2
                    o = o_t[b % 2]
                    yield first + 1
                    k = sp.dma(sums[:], o[HD:HD + 97:32, :].rearrange("i (q n) -> i q n", n=sums.shape[1]), s_sums,
                               pv_done[b, GROUPS - 1], state["recip"])
                    yield first + 4
                    rk = dve.do(lambda q: q.reciprocal(recip[:], sums[:]), k, state["recip"])
                    yield first + 5
                    state["recip"] = k = sp.dma(recip_d.rearrange("i (q n) -> (i q) n", n=sums.shape[1]), recip[:], s_recip, rk,
                                                state["recip_b"])
                    yield first + 7
                    bk = sp.dma(recip_b[:], recip_d.rearrange("i (o n) -> i o n", o=1).broadcast_to([PV_HEADS, 32, GROUPS * N]),
                                s_recip_in, k, state["recip_b"])
                    gate_ok = sp.dma(gate[:], mod_d[l, b:b + 1, 2 * C:3 * C].broadcast_to([P, C]), s_gate, state["gate_free"],
                                     prepared["mod", l])
                    yield first + 11
                    half = GROUPS * N // 2
                    nk = []
                    for j in range(2):
                        cols = slice(half * j, half * j + half)
                        nk.append(tt(dve, o[:, cols], o[:, cols], recip_b[:, cols], ALU.mult, bk))
                        if j == 0:
                            yield first + 12
                    state["recip_b"] = nk[-1]
                    for t, (slot, second) in enumerate(PROJ_SLOTS):
                        yield HEADS * b + slot
                        bank = take()

                        def project(groups, t=t, bank=bank):
                            def emit(q):
                                for g in groups:
                                    last = q.matmul(bank.ap[:, 0:C], o[:, g * N + t * P:g * N + t * P + P], w_proj[:, g, :],
                                                    start=(g == 0), stop=(g == GROUPS - 1))
                                return last
                            return pe.do(emit, nk, w_ok, bank.free)

                        project(range(GROUPS // 2))
                        yield HEADS * b + second
                        mm = project(range(GROUPS // 2, GROUPS))
                        yield gate_and_add(b, t, bank, mm, HEADS * b + second, gate_ok)
                    o_free[b % 2] = mm

                def gate_and_add(b, t, bank, mm, slot, gate_ok):
                    yield slot + 1
                    gk = state["gate_free"] = put(bank, tt(dve, gated[:], bank.ap[:, 0:C], gate[:], ALU.mult, mm, gate_ok,
                                                           state["gated"]))
                    yield slot + 2
                    xt = x_sb[:, TT * b + t, :]
                    x_marks[TT * b + t] = state["gated"] = tt(pool, xt, xt, gated[:], ALU.add, gk)

                agenda = Agenda(FRONT_START)
                maxima = exps = None
                for T in range(FRONT_START, HEADS * B + PROJ_SLOTS[-1][1] + 3):
                    b, h = divmod(T, HEADS)
                    if exps:
                        exponentials(*exps)
                    if maxima:
                        reduce_max(*maxima)
                        if maxima[1] == HEADS - 1:
                            agenda.start(place_maxima(maxima[0]))
                    mb, mh = divmod(T + MAX_LEAD, HEADS)
                    maxima = (mb, mh, max_scores(mb, mh)) if 0 <= mb < B else None
                    exps = (b, h, shifted_scores(b, h)) if 0 <= b < B else None
                    fb, fh = divmod(T - FRONT_START, HEADS)
                    if fh == 0 and fb < B:
                        agenda.start(front(fb), last=True)
                    agenda.run(T)
                    vb, vh = divmod(T - 2, HEADS)
                    if 0 <= vb < B and vh % PV_HEADS == PV_HEADS - 1:
                        agenda.start(values(vb, vh // PV_HEADS, T))
                for bk in psum:
                    bk.free = None
            return run

        CHUNKS = MLP // P
        SLOTS = CHUNKS + 6

        def mlp(l):
            def run(sb):
                banks = Banks(psum)
                take, put = banks.take, banks.put

                w1 = sb("w_fc1_stacked", [P, WIDE_CHUNKS, MLP], F32R)
                w2 = {part: sb(f"w_fc2_{part}", [P, CHUNKS, C], F32R) for part in ("hi", "lo")}
                ln = Normaliser(sb, 2)
                mod = [sb(f"scale_shift{i}", [P, 2 * C]) for i in range(2)]
                gate = [sb(f"gate_and_gated_bias{i}", [P, 2 * C]) for i in range(2)]
                hidden = [sb(f"hidden{i}", [P, N]) for i in range(3)]
                h_hi = [sb(f"hidden_hi{i}", [P, CHUNKS, N], F32R) for i in range(2)]
                h_lo = [sb(f"hidden_lo{i}", [P, CHUNKS, N], F32R) for i in range(2)]
                gated = [sb(f"gated{i}", [P, C]) for i in range(TT)]
                mod_free, gate_free, h_free, gated_free = [None] * 2, [None] * 2, [None] * 2, [None] * TT
                hidden_free = [None] * 3
                chunks_done = [0]
                w1_ok, w2_ok, h_split = {}, [], {}
                scratch_w = h_lo[1][:].rearrange("p m n -> p (m n)")

                def front(b):
                    i, start = b % 2, SLOTS * b - SLOTS
                    mod_ok = sp.dma(mod[i][:], mod_d[l, b:b + 1, 3 * C:5 * C].broadcast_to([P, 2 * C]), s_mod2[i], mod_free[i],
                                    prepared["mod", l])
                    yield start + 2
                    yield from ln.run(b, start + 2, mod[i][:, 0:C], mod[i][:, C:2 * C], mod_ok, take, put)
                    mod_free[i] = ln.mod_read

                def fc1(b):
                    i, start = b % 2, SLOTS * b
                    xt, xt_ok = ln.ready
                    h_split[b] = []
                    for m in range(CHUNKS):
                        yield start + m
                        bank = take()
                        if b == 0 and m * P % group == 0:
                            g = m * P // group
                            w1_ok[g] = split_stacked(w1, w1, slice(group * g, group * (g + 1)), scratch_w, w1_loaded[g])
                        mm = matmuls(wide_steps(bank.ap[:, 0:N], w1, xt, (m * P, m * P + P), (0, N), True), xt_ok,
                                     w1_ok[m * P // group], bank.free)
                        yield activate(b, m, bank, mm, start + m)
                    ln.xt_free[i] = mm

                def activate(b, m, bank, mm, slot):
                    i, r = b % 2, chunks_done[0] % 3
                    chunks_done[0] += 1
                    yield slot + 1
                    gk = put(bank, func(hidden[r][:], bank.ap[:, 0:N], ACT.Gelu_apprx_tanh, mm, hidden_free[r]))
                    yield slot + 2
                    after = [h_free[i]] + (w1_ok[FC1_LOADS - 1] if b == 1 else [])
                    hk = copy(dve, h_hi[i][:, m, :], hidden[r][:], gk, after)
                    lk = hidden_free[r] = tt(dve, h_lo[i][:, m, :], hidden[r][:], fp(h_hi[i][:, m, :]), ALU.subtract, hk, after)
                    h_split[b] += [hk, lk]

                def fc2(b):
                    i, start = b % 2, SLOTS * b + SLOTS + CHUNKS
                    yield start - 5
                    gate_ok[b] = sp.dma(gate[i][:], mod_d[l, b:b + 1, 5 * C:7 * C].broadcast_to([P, 2 * C]), s_gate2[i],
                                        gate_free[i], prepared["mod", l])
                    yield start
                    for t in range(TT):
                        bank = take()
                        cols = slice(t * P, t * P + P)
                        for third in range(3):
                            yield start + 3 * t + third

                            def emit(q, bank=bank, cols=cols, third=third):
                                for c in range(3 * third, 3 * third + 3):
                                    for x, w in ((h_hi, "hi"), (h_hi, "lo"), (h_lo, "hi")):
                                        last = q.matmul(bank.ap[:, 0:C], x[i][:, c, cols], w2[w][:, c, :],
                                                        start=(c == 0 and x is h_hi and w == "hi"),
                                                        stop=(c == CHUNKS - 1 and x is h_lo))
                                return last
                            mm = pe.do(emit, h_split[b], w2_ok, bank.free)
                        yield gate_and_add(b, t, bank, mm, start + 3 * t + 2)
                    h_free[i] = mm

                def gate_and_add(b, t, bank, mm, slot):
                    i = b % 2
                    yield slot + 1
                    gk = put(bank, tt(dve, gated[t][:], bank.ap[:, 0:C], gate[i][:, 0:C], ALU.mult, mm, gate_ok[b], gated_free[t]))
                    yield slot + 2
                    xt = x_sb[:, TT * b + t, :]
                    k = gated_free[t] = tt(pool, xt, xt, gated[t][:], ALU.add, gk)
                    k = x_marks[TT * b + t] = gate_free[i] = tt(pool, xt, xt, gate[i][:, C:2 * C], ALU.add, k)
                    if t == TT - 1 and l == LAYERS - 1:
                        yield slot + 4
                        sp.dma(out[b].rearrange("(t p) c -> p t c", p=P), x_sb[:, TT * b:TT * b + TT, :], s_out, k)

                gate_ok = {}
                agenda = Agenda(-SLOTS)
                for T in range(-SLOTS, SLOTS * (B + 1) + 6):
                    b, s = divmod(T, SLOTS)
                    if s == 0:
                        if b + 1 < B:
                            agenda.start(front(b + 1))
                        if b == -1:
                            w1_loaded = [load_stacked(w1, fc1_d[l][g], slice(group * g, group * (g + 1)), s_w_fc1[g], prepared["fc1", l])
                                         for g in range(FC1_LOADS)]
                            w2_raw = sp.dma(fp(w2["lo"][:]), fc2_d[l], s_w_fc2, prepared["fc2", l])
                        if 0 <= b < B:
                            agenda.start(fc1(b))
                            agenda.start(fc2(b))
                        if b == 2 and l + 1 < LAYERS:
                            raw_ok = load_stacked(w_attn, qkv_d, slice(0, 3 * C), s_w, prepared["qkv", 1])
                        if b == 4 and l + 1 < LAYERS:
                            split_ok = split_stacked(w_attn, w_attn, slice(0, 3 * C), proj_space, raw_ok)
                            prepared["attn_weights", l + 1] = split_ok + load_proj(l + 1, split_ok)
                    if T == CHUNKS:
                        w2_ok.append(copy(act, w2["hi"][:], fp(w2["lo"][:]), w2_raw))
                        w2_ok.append(tt(dve, w2["lo"][:], fp(w2["lo"][:]), fp(w2["hi"][:]), ALU.subtract, w2_ok[0]))
                    agenda.run(T)
                for bk in psum:
                    bk.free = None
            return run

        phase("prep", prepare)
        for l in range(LAYERS):
            phase(f"attn{l}", attention(l))
            phase(f"mlp{l}", mlp(l))

        block = outer.enter_context(nc.Block())
        block.tensor(pe.play)
        block.scalar(act.play)
        block.vector(dve.play)
        block.gpsimd(pool.play)
        block.sync(sp.play)


_INS = ['x', 'cond_1152', 'L0_cond_w_mod', 'L0_cond_b_mod', 'L0_cond_w_qkv', 'L0_cond_b_qkv', 'L0_cond_g_q', 'L0_cond_g_k',
        'L0_cond_w_proj', 'L0_cond_b_proj', 'L0_cond_w1', 'L0_cond_b1', 'L0_cond_w2', 'L0_cond_b2',
        'L1_cond_W_qkv', 'L1_cond_b_qkv', 'L1_cond_W_proj', 'L1_cond_b_proj', 'L1_cond_W_fc1', 'L1_cond_b_fc1',
        'L1_cond_W_fc2', 'L1_cond_b_fc2', 'L1_cond_W_ada', 'L1_cond_b_ada']


def kernel(**inputs):
    import numpy as _np
    import concourse.bacc as _bacc
    from concourse import mybir as _mybir
    from concourse.bass_utils import run_bass_kernel_spmd as _run

    nc = _bacc.Bacc("TRN2", target_bir_lowering=False, num_devices=1, dynamic_dma_scratch_size=64)
    arrays, aps = {}, {}
    for name in _INS:
        v = _np.ascontiguousarray(inputs[name])
        arrays[f"in_{name}_dram"] = v
        aps[name] = nc.dram_tensor(f"in_{name}_dram", v.shape, _mybir.dt.from_np(v.dtype), kind="ExternalInput").ap()
    out = nc.dram_tensor("out_0_dram", (B, N, C), F32, kind="ExternalOutput").ap()
    build(nc, aps, out)
    r = _run(nc, [arrays], core_ids=[0])
    return r.results[0]["out_0_dram"]
```

```python
from contextlib import ExitStack

import concourse.bass as bass
from concourse import mybir

F32 = mybir.dt.float32
F32R = mybir.dt.float32r
BF16 = mybir.dt.bfloat16
ALU = mybir.AluOpType
ACT = mybir.ActivationFunctionType
AX = mybir.AxisListType

B, N, C = 32, 256, 288
HEADS = 16
HD = C // HEADS
MLP = 4 * C
FC1_LOADS = 3
LAYERS = 2
MLP_WEIGHTS = (("L0_cond_w1", "L0_cond_b1", "L0_cond_w2"), ("L1_cond_W_fc1", "L1_cond_b_fc1", "L1_cond_W_fc2"))
X_LOADS = 8
P = 128
TT = N // P
EPS = 1e-6
SCORE_SCALE = float(HD) ** -0.5
K3 = C // 3

XS_COLS = 2 * C + 32
WIDE_ROWS = [128, 128, 128, 128, 98]
WIDE_CHUNKS = 7
WIDE_PAIRS = [(0, 0), (1, 1), (2, 2), (3, 3), (4, 4), (5, 0), (6, 1)]

QK = 2 * C
QK_M = 7 * HD
QK_CHUNKS = [(m, min(QK_M, QK - m)) for m in range(0, QK, QK_M)]
STACK = 6 * HD
VW = HD + 2
PV_HEADS = 4
GROUPS = HEADS // PV_HEADS

STACK_RING, V_RING, P_RING, PSUM_RING = 3, 5, 6, 3
Z_RING, PARTS_RING = 4, 4

MAX_LEAD = HEADS + 8
REST_SLOTS = 16
FC1_LOAD_SLOTS = [-12, -6, -2]
FC1_SPLIT_SLOTS = [-12, -8, -4]
FC2_LOAD_SLOT = -6
ONES_SLOTS = [17, 27, 33]
FRONT_START = -79
CHUNK_SLOTS = [-57, -56, -54, -53, -52]
VALUE_SLOTS = [-50, -49]
STACKS_SLOT = -32
PROJ_SLOTS = [(32, 34), (36, 37)]


class Engine:

    def __init__(self, sem):
        self.sem, self.count, self.queue, self.seen = sem, 0, [], {}

    def wait(self, *after):
        for mark in flat(after):
            sem, value = mark
            if self.seen.get(id(sem), 0) < value:
                self.seen[id(sem)] = value
                self.queue.append(lambda e, s=sem, v=value: e.wait_ge(s, v))

    def do(self, emit, *after):
        self.wait(*after)
        self.count += 1
        self.queue.append(lambda e, f=emit: f(e).then_inc(self.sem, 1))
        return (self.sem, self.count)

    def dma(self, out, in_, stream, *after):
        self.wait(*after)
        stream.count += 16
        self.queue.append(lambda e, s=stream.sem: e.dma_start(out, in_).then_inc(s, 16))
        return (stream.sem, stream.count)

    def play(self, e):
        for step in self.queue:
            step(e)


class Stream:

    def __init__(self, sem):
        self.sem, self.count = sem, 0


def flat(marks):
    for m in marks:
        if m is None:
            continue
        if isinstance(m, list):
            yield from flat(m)
        else:
            yield m


class Bank:

    def __init__(self, ap):
        self.ap, self.free = ap, None


class Banks:

    def __init__(self, banks):
        self.idle = list(banks)

    def take(self):
        return self.idle.pop(0)

    def put(self, bank, mark):
        bank.free = mark
        self.idle.append(bank)
        return mark


class Agenda:

    def __init__(self, slot):
        self.slot, self.started, self.waiting = slot, 0, []

    def start(self, g, last=False):
        self.started += 1
        self.step((last, self.started), g)

    def step(self, age, g):
        for then in g:
            if isinstance(then, int):
                if then > self.slot:
                    self.waiting.append((age, then, g))
                    return
            else:
                self.start(then)

    def run(self, slot):
        self.slot = slot
        due = sorted((w for w in self.waiting if w[1] <= slot), key=lambda w: w[0])
        self.waiting = [w for w in self.waiting if w[1] > slot]
        for age, _, g in due:
            self.step(age, g)


def build(nc, a, out):
    outer = ExitStack()
    with outer:
        def sem(name):
            return outer.enter_context(nc.semaphore(name))

        def stream(name):
            return Stream(sem(name))

        pe, act, dve, pool, sp = (Engine(sem(n)) for n in ("pe_done", "act_done", "dve_done", "pool_done", "sp_unused"))
        engines = [pe, act, dve, pool, sp]

        def sb_in(scope, name, shape, dt=F32):
            return scope.enter_context(nc.sbuf_tensor(name, shape, dt))

        def phase(name, build_phase, *before):
            with ExitStack() as scope:
                return build_phase(lambda n, shape, dt=F32: sb_in(scope, f"{name}_{n}", shape, dt), *before)

        def meet(*who):
            marks = [(e.sem, e.count) for e in engines if e.count]
            marks += [(s.sem, s.count) for s in streams if s.count]
            for e in who or engines:
                e.wait(marks)

        def rest_of(agenda, slot):
            def step():
                nonlocal slot
                agenda.run(slot)
                slot += 1
                return step if agenda.waiting else None
            return step

        streams = []

        def new_stream(name):
            s = stream(name)
            streams.append(s)
            return s

        x_sb = sb_in(outer, "x_resident", [P, B * TT, C])
        ident_wide = sb_in(outer, "identity_between_zeros", [P, 3 * P], F32R)
        ident = ident_wide[:, P:2 * P].bitcast(F32)
        head_ones = sb_in(outer, "head_block_ones", [P, P])
        minus_half = sb_in(outer, "minus_half", [P, TT])
        minus_lo_row = sb_in(outer, "minus_one_on_low_rows", [P, 1])
        eps_col = sb_in(outer, "eps_column", [P, 1])
        qk_gain = sb_in(outer, "qk_gain", [P, len(QK_CHUNKS)])
        w_attn = sb_in(outer, "w_qkv_stacked", [P, WIDE_CHUNKS, 3 * C], F32R)
        w_proj = sb_in(outer, "w_proj_by_heads", [P, GROUPS, C])
        psum = [Bank(outer.enter_context(nc.psum_tensor(f"psum{i}", [P, 512], F32))) for i in range(8)]

        def scratch(name, shape, dt=F32):
            return nc.dram_tensor(name, shape, dt).ap()

        mod_d = scratch("modulation", (LAYERS, B, 7 * C))
        group = MLP // FC1_LOADS
        qkv_d = scratch("qkv_stacked", (P, WIDE_CHUNKS, 3 * C))
        fc1_d = [[scratch(f"fc1_stacked_{l}_{g}", (P, WIDE_CHUNKS, group)) for g in range(FC1_LOADS)] for l in range(LAYERS)]
        fc2_d = [scratch(f"fc2_by_rows_{l}", (P, MLP // P, C)) for l in range(LAYERS)]
        parts_d = [scratch(f"qk_parts_{i}", (3, QK, N), BF16) for i in range(2)]
        recip_d = scratch("row_reciprocals", (PV_HEADS, GROUPS * N))

        s_x = [stream(f"x_loaded_{i}") for i in range(X_LOADS)]
        s_out = new_stream("out_stored")
        s_gain = new_stream("gains_loaded")
        s_cond = new_stream("cond_loaded")
        s_w_mod = [new_stream(f"w_mod_loaded_{l}") for l in range(LAYERS)]
        s_mod_rows = [new_stream(f"mod_rows_stored_{l}") for l in range(LAYERS)]
        s_w = new_stream("attn_weights_loaded")
        s_w_proj = stream("proj_weights_loaded")
        s_w_fc1 = [new_stream(f"fc1_weights_loaded_{i}") for i in range(FC1_LOADS)]
        s_w_fc2 = new_stream("fc2_weights_loaded")
        s_order_fc1 = [stream(f"fc1_arranged_{l}") for l in range(LAYERS)]
        s_order_fc2 = [stream(f"fc2_arranged_{l}") for l in range(LAYERS)]
        s_order_qkv = stream("qkv_arranged")
        s_mod = new_stream("attn_mod_loaded")
        s_gate = new_stream("attn_gate_loaded")
        s_mod2 = [new_stream(f"mlp_mod_loaded_{i}") for i in range(2)]
        s_gate2 = [new_stream(f"mlp_gate_loaded_{i}") for i in range(2)]
        s_parts = [new_stream(f"parts_stored_{m}") for m in range(len(QK_CHUNKS))]
        s_stack = [new_stream(f"stack_loaded_{i}") for i in range(STACK_RING)]
        s_max = new_stream("maxima_placed")
        s_sums = new_stream("sums_spread")
        s_recip = new_stream("reciprocals_stored")
        s_recip_in = new_stream("reciprocals_loaded")

        def copy(e, out_, in_, *after):
            if e is act:
                return e.do(lambda q: q.activation(out_, in_, ACT.Copy), *after)
            return e.do(lambda q: q.tensor_copy(out_, in_), *after)

        def tt(e, out_, in0, in1, op, *after):
            return e.do(lambda q: q.tensor_tensor(out_, in0, in1, op), *after)

        def stt(out_, in0, scalar, in1, op0, op1, *after):
            return dve.do(lambda q: q.scalar_tensor_tensor(out=out_, in0=in0, scalar=scalar, in1=in1, op0=op0, op1=op1), *after)

        def func(out_, in_, f, *after, **kw):
            return act.do(lambda q: q.activation(out_, in_, f, **kw), *after)

        def matmuls(steps, *after):
            def emit(q):
                last = None
                for i, (o, l, r) in enumerate(steps):
                    last = q.matmul(o, l, r, start=(i == 0), stop=(i == len(steps) - 1))
                return last
            return pe.do(emit, *after)

        def fp(ap):
            return ap.bitcast(F32)

        def wide_steps(out_, weights, acts, w_cols, a_cols, weights_stationary):
            steps = []
            for kw, ka in WIDE_PAIRS:
                rows = WIDE_ROWS[ka]
                w = weights[0:rows, kw, w_cols[0]:w_cols[1]]
                x = acts[0:rows, ka, a_cols[0]:a_cols[1]]
                steps.append((out_, w, x) if weights_stationary else (out_, x, w))
            return steps

        draft = w_proj[:].rearrange("p g n -> p (g n)")[:, 0:3 * P]
        k = dve.do(lambda q: q.memset(draft, 0.0))
        k = pool.do(lambda q: q.affine_select(out=draft, in_=draft, compare_op=ALU.not_equal, fill=1.0,
                                              base=P, pattern=[[-1, 3 * P]], channel_multiplier=1), k)
        ident_ok = copy(dve, ident_wide[:], draft, k)
        k = dve.do(lambda q: q.memset(head_ones[:], 1.0))
        blocks = head_ones[:, 0:QK_M].rearrange("p (j d) -> p j d", d=HD)
        k = pool.do(lambda q: q.affine_select(out=blocks, in_=blocks, compare_op=ALU.is_ge, fill=0.0,
                                              base=0, pattern=[[-HD, 7], [0, HD]], channel_multiplier=1), k)
        head_ones_ok = pool.do(lambda q: q.affine_select(out=blocks, in_=blocks, compare_op=ALU.is_ge, fill=0.0,
                                                         base=HD - 1, pattern=[[HD, 7], [0, HD]], channel_multiplier=-1), k)
        dve.do(lambda q: q.memset(eps_col[:], EPS))
        k = dve.do(lambda q: q.memset(minus_lo_row[:], -1.0))
        k = dve.do(lambda q: q.memset(minus_lo_row[0:64, :], 0.0), k)
        dve.do(lambda q: q.memset(minus_lo_row[96:97, :], 0.0), k)
        dve.do(lambda q: q.memset(minus_half[:], -0.5))
        const_ok = (dve.sem, dve.count)

        gk_col = sb_in(outer, "g_k_columns", [P, len(QK_CHUNKS)])
        dve.do(lambda q: q.memset(qk_gain[:], 1.0))
        const_gain = dve.do(lambda q: q.memset(gk_col[:], 1.0))
        for m, (c0, rows) in enumerate(QK_CHUNKS):
            n = min(rows, C - c0) // HD
            if n > 0:
                for dst, g in ((qk_gain, "L0_cond_g_q"), (gk_col, "L0_cond_g_k")):
                    gains_loaded = act.dma(dst[0:n * HD, m:m + 1], a[g].rearrange("(o d) -> o d", o=1).broadcast_to([n, HD]),
                                           s_gain, const_gain)

        prepared, x_marks = {}, {}

        def prepare(sb):
            cond = sb("cond", [B, C])
            silu_a = sb("silu_denominator", [B, C])
            silu_b = sb("silu", [B, C])
            silu_t = sb("silu_transposed", [K3, 3, B])
            loaded = sp.dma(cond[:], a["cond_1152"], s_cond)
            k = func(silu_a[:], cond[:], ACT.Exp, loaded, scale=-1.0)
            k = dve.do(lambda q: q.tensor_scalar(silu_a[:], silu_a[:], 1.0, None, ALU.add), k)
            k = dve.do(lambda q: q.reciprocal(silu_a[:], silu_a[:]), k)
            silu_ok = tt(dve, silu_b[:], cond[:], silu_a[:], ALU.mult, k)
            for i in range(3):
                t = pe.do(lambda q, i=i: q.transpose(psum[i].ap[0:K3, 0:B], silu_b[:, K3 * i:K3 * i + K3], ident[0:B, 0:B]),
                          silu_ok, ident_ok)
                silu_t_ok = psum[i].free = copy(dve, silu_t[:, i, :], psum[i].ap[0:K3, 0:B], t)
            w_mod = [sb(f"w_mod{l}", [K3, 3, 6 * C]) for l in range(LAYERS)]
            b_mod = [sb(f"b_mod{l}", [B, 6 * C]) for l in range(LAYERS)]
            b_2 = [sb(f"b_fc2_{l}", [B, C]) for l in range(LAYERS)]
            rows = [sb(f"mod_rows{l}", [B, 7 * C]) for l in range(LAYERS)]
            order = [1, 0, 2, 4, 3, 5]
            names = (("L0_cond_w_mod", "L0_cond_b_mod", "L0_cond_b2"), ("L1_cond_W_ada", "L1_cond_b_ada", "L1_cond_b_fc2"))

            def load_modulation(l):
                w, bias, b2 = names[l]
                sp.dma(w_mod[l][:], a[w].rearrange("(i p) n -> p i n", p=K3), s_w_mod[l])
                sp.dma(b_mod[l][:], a[bias].rearrange("(o n) -> o n", o=1).broadcast_to([B, 6 * C]), s_w_mod[l])
                return sp.dma(b_2[l][:], a[b2].rearrange("(o n) -> o n", o=1).broadcast_to([B, C]), s_w_mod[l])

            def modulation(l, loaded):
                done = []
                for j in range(6):
                    bank = psum[3 + j % 5]
                    mm = matmuls([(bank.ap[0:B, 0:C], silu_t[:, i, :], w_mod[l][:, i, C * j:C * j + C]) for i in range(3)],
                                 loaded, silu_t_ok, bank.free)
                    to = order.index(j)
                    r = bank.free = stt(rows[l][:, C * to:C * to + C], bank.ap[0:B, 0:C], 1.0 if j in (1, 4) else 0.0,
                                        b_mod[l][:, C * j:C * j + C], ALU.add, ALU.add, mm, loaded)
                    done.append(r)
                g = tt(dve, rows[l][:, 6 * C:7 * C], rows[l][:, 5 * C:6 * C], b_2[l][:], ALU.mult, done)
                prepared["mod", l] = sp.dma(mod_d[l], rows[l][:], s_mod_rows[l], g)

            mod_loaded = load_modulation(0)
            def load_x(g):
                n = B // X_LOADS
                mark = sp.dma(x_sb[:, TT * n * g:TT * n * (g + 1), :],
                               a["x"][n * g:n * (g + 1)].rearrange("b (t p) c -> p (b t) c", p=P), s_x[g])
                for i in range(TT * n * g, TT * n * (g + 1)):
                    x_marks[i] = mark
            load_x(0)
            raw = sb("raw_qkv", [P, len(WIDE_ROWS), 3 * C])
            arrange_stacked(("qkv", 0), raw, "L0_cond_w_qkv", "L0_cond_b_qkv", slice(0, 3 * C), s_w, len(WIDE_ROWS))
            raw_ok = prepared["qkv", 0]
            mod_1_loaded = load_modulation(1)
            modulation(0, mod_loaded)

            centred = []
            for c0, c1, n in ((0, 4, P), (4, 5, WIDE_ROWS[4])):
                means = sb(f"head_means_{c0}", [P, c1 - c0, 2 * HEADS])
                m = means[0:n, :, :]
                qk = raw[0:n, c0:c1, 0:QK].rearrange("p c (h d) -> p c h d", d=HD)
                k = dve.do(lambda q, m=m, qk=qk: q.tensor_reduce(m, qk, AX.X, ALU.add), raw_ok)
                k = dve.do(lambda q, m=m: q.tensor_scalar(m, m, -1.0 / HD, None, ALU.mult), k)
                mb = m.rearrange("p c (h o) -> p c h o", o=1).broadcast_to([n, c1 - c0, 2 * HEADS, HD])
                centred.append(tt(dve, qk, qk, mb, ALU.add, k))
            modulation(1, mod_1_loaded)
            tt(dve, qk_gain[:], qk_gain[:], gk_col[:], ALU.mult, gains_loaded)
            split_ok = split_stacked(raw, w_attn, slice(0, 3 * C), proj_space, centred + [raw_ok])
            prepared["attn_weights", 0] = split_ok + load_proj(0, split_ok)
            for g in range(1, X_LOADS):
                deferred.append((load_x, g))
            for l in range(LAYERS):
                w1, b1, w2 = MLP_WEIGHTS[l]
                for g in range(FC1_LOADS):
                    deferred.append((arrange_stacked, ("fc1", l), fc1_d[l][g], w1, b1, slice(group * g, group * (g + 1)),
                                     s_order_fc1[l]))
                deferred.append((arrange, ("fc2", l), fc2_d[l], a[w2].rearrange("(c p) n -> p c n", p=P), s_order_fc2[l]))
                if l == 0:
                    deferred.append((arrange_stacked, ("qkv", 1), qkv_d, "L1_cond_W_qkv", "L1_cond_b_qkv", slice(0, 3 * C),
                                     s_order_qkv))

        deferred = []

        def arrange(name, dst, src, st):
            prepared[name] = sp.dma(dst, src, st)

        proj_space = w_proj[:].rearrange("p g n -> p (g n)").bitcast(F32R)

        def arrange_stacked(name, dst, w, bias, cols, st, chunks=WIDE_CHUNKS):
            w, bias = a[w][:, cols], a[bias].rearrange("(o n) -> o n", o=1)[:, cols]
            moves = [
                (dst[:, 0:2, :], w[0:256, :].rearrange("(i p) n -> p i n", p=P)),
                (dst[0:32, 2, :], w[256:288, :]), (dst[32:128, 2, :], w[0:96, :]),
                (dst[:, 3, :], w[96:224, :]),
                (dst[0:64, 4, :], w[224:288, :]), (dst[64:96, 4, :], w[256:288, :]),
                (dst[96:98, 4, :], bias.broadcast_to([2, cols.stop - cols.start])),
            ]
            if chunks == WIDE_CHUNKS:
                moves.append((dst[:, 5:7, :], w[0:256, :].rearrange("(i p) n -> p i n", p=P)))
            for d, s in moves:
                prepared[name] = sp.dma(d, s, st)

        def load_stacked(dst, src, cols, st, *after):
            rows = WIDE_ROWS[4]
            sp.dma(fp(dst[:, 0:4, cols]), src[:, 0:4, :], st, *after)
            sp.dma(fp(dst[0:rows, 4, cols]), src[0:rows, 4, :], st, *after)
            return sp.dma(fp(dst[:, 5:7, cols]), src[:, 5:7, :], st, *after)

        def split_stacked(src, dst, cols, tmp, *loaded):
            rows = WIDE_ROWS[4]
            mixed, low = dst[0:rows, 4, cols], dst[:, 5:7, cols]
            t = tmp[0:rows, 0:cols.stop - cols.start]
            hk = copy(act, dst[:, 0:4, cols], fp(src[:, 0:4, cols]), *loaded)
            tk = copy(act, t, fp(src[0:rows, 4, cols]), *loaded)
            low_src = src[:, 5:7, cols] if src is dst else src[:, 0:2, cols]
            lk = tt(dve, low, fp(low_src), fp(dst[:, 0:2, cols]), ALU.subtract, hk, *loaded)
            mk = stt(mixed, fp(t), minus_lo_row[0:rows, :], fp(src[0:rows, 4, cols]), ALU.mult, ALU.add, tk, const_ok, *loaded)
            return [hk, tk, lk, mk]

        def load_proj(l, *after):
            zero = dve.do(lambda q: q.memset(w_proj[:], 0.0), *after)
            wp, bp = (("L0_cond_w_proj", "L0_cond_b_proj"), ("L1_cond_W_proj", "L1_cond_b_proj"))[l]
            by_head = a[wp].rearrange("(g i d) n -> i d g n", i=PV_HEADS, d=HD)
            for i in range(PV_HEADS):
                sp.dma(w_proj[32 * i:32 * i + HD, :, :], by_head[i], s_w_proj, zero)
            mark = sp.dma(w_proj[HD:HD + 1, 0, :], a[bp].rearrange("(o n) -> o n", o=1), s_w_proj, zero)
            return [mark]

        class Normaliser:

            def __init__(self, sb, ring):
                self.stats = sb("ln_stats", [P, TT, 6])
                self.mv = sb("ln_mean_var", [P, TT, 2])
                self.rstd = sb("ln_rstd", [P, TT])
                self.scaled = sb("ln_scaled", [P, C])
                self.y = [sb(f"ln_modulated{i}", [P, C]) for i in range(2)]
                self.xs = [sb(f"ln_split{i}", [P, XS_COLS], F32R) for i in range(TT)]
                self.xt = [sb(f"ln_transposed{i}", [P, len(WIDE_ROWS), N], F32R) for i in range(ring)]
                self.xt_free = [None] * ring
                self.xs_free = [None] * TT
                self.stats_free = self.mv_free = self.rstd_free = self.scaled_free = None
                self.y_free = [None, None]
                self.mod_read = None
                self.ones_ok = [dve.do(lambda q, t=t: q.memset(fp(t[96:98, 4, :]), 1.0)) for t in self.xt]

            def run(self, b, start, transposes, scale_row, shift_row, mod_ok, take, put):
                hi_cols, lo_cols, dup = slice(0, C), slice(C, 2 * C), slice(2 * C, XS_COLS)
                ring = b % len(self.xt)
                agg = []
                for t in range(TT):
                    xt = x_sb[:, TT * b + t, :]
                    st = dve.do(lambda q, t=t, xt=xt: q.bn_stats(self.stats[:, t, :], xt), x_marks[TT * b + t], self.stats_free)
                    agg.append(dve.do(lambda q, t=t: q.bn_aggr(self.mv[:, t, :], self.stats[:, t, :]), st, self.mv_free))
                    yield start + 1 + t
                self.stats_free = agg
                k = pool.do(lambda q: q.tensor_scalar(self.rstd[:], self.mv[:, :, 1], EPS, None, ALU.add), agg, self.rstd_free)
                rstd_ok = tt(pool, self.rstd[:], self.rstd[:], minus_half[:, 0:TT], ALU.pow, k, const_ok)
                yield start + 3
                done = []

                def modulate(t):
                    u = stt(self.scaled[:], x_sb[:, TT * b + t, :], self.mv[:, t, 0:1], scale_row, ALU.subtract, ALU.mult,
                            agg, mod_ok, self.scaled_free)
                    y = self.scaled_free = stt(self.y[t][:], self.scaled[:], self.rstd[:, t:t + 1], shift_row, ALU.mult, ALU.add,
                                               u, rstd_ok, self.y_free[t])
                    return y

                def high(t, y):
                    return copy(act, self.xs[t][:, hi_cols], self.y[t][:], y, self.xs_free[t])

                def low(t, h):
                    xs = self.xs[t]
                    lo = tt(pool, xs[:, lo_cols], self.y[t][:], fp(xs[:, hi_cols]), ALU.subtract, h, self.xs_free[t])
                    self.y_free[t] = [h, lo]
                    d = copy(pool, xs[:, dup], fp(xs[:, 256:C]), h, self.xs_free[t])
                    done.append([h, lo, d])

                y0 = modulate(0)
                yield start + 4
                y1 = modulate(1)
                self.mv_free = self.rstd_free = self.mod_read = y1
                h0 = high(0, y0)
                yield start + 5
                h1 = high(1, y1)
                low(0, h0)
                yield start + 6
                low(1, h1)
                yield transposes
                evac = []
                pending = None
                for n, pair in enumerate(((0, 1), (2, 3), (4,), None)):
                    if pending:
                        tr, bank, rows, c0, n_c = pending
                        evac.append(copy(act, self.xt[ring][0:rows, c0:c0 + n_c, :],
                                         bank.ap[0:rows, 0:n_c * N].rearrange("p (c n) -> p c n", c=n_c), tr,
                                         self.xt_free[ring], self.ones_ok[ring]))
                        put(bank, evac[-1])
                    if pair is None:
                        break
                    bank = take()
                    rows = 96 if pair == (4,) else P

                    def emit(q, pair=pair, bank=bank, rows=rows):
                        for j, c in enumerate(pair):
                            for t in range(TT):
                                last = q.matmul(bank.ap[0:rows, j * N:j * N + N], self.xs[t][:, c * P:c * P + rows],
                                                ident_wide[:, P - t * P:P - t * P + N], start=(t == 0), stop=(t == TT - 1))
                        return last
                    tr = pe.do(emit, done, bank.free, ident_ok)
                    pending = (tr, bank, rows, pair[0], len(pair))
                    self.xs_free = [tr] * TT
                    yield transposes + 1 + n
                self.ready = (self.xt[ring], evac)


        w1_here = []

        def attention(l):
            def run(sb, rest_before):
                with ExitStack() as early:
                    w1 = sb_in(early, f"w_fc1_stacked_{l}", [P, WIDE_CHUNKS, MLP], F32R)
                w1_here.append((w1, []))
                banks = Banks(psum[8 - PSUM_RING:])
                take, put = banks.take, banks.put

                ln = Normaliser(sb, 1)
                mod = sb("scale_shift", [P, 2 * C])
                parts = [sb(f"qk_parts{i}", [P, 3, N], BF16) for i in range(PARTS_RING)]
                rest = [sb(f"qk_rest{i}", [P, N]) for i in range(2)]
                if l == 0:
                    z_sb = [sb(f"qk_centred{i}", [P, N]) for i in range(Z_RING)]
                    sq_sb = [sb(f"qk_squares{i}", [P, N]) for i in range(2)]
                    rstd_sb = [sb(f"qk_rstd{i}", [P, N]) for i in range(2)]
                else:
                    sb("room_of_the_head_norm", [P, (Z_RING + 4) * N])
                maxes = [sb(f"maxima{i}", [P, HEADS, TT]) for i in range(2)]
                q_st = [sb(f"q_stack{i}", [P, HEADS, N], BF16) for i in range(STACK_RING)]
                k_st = [sb(f"k_stack{i}", [P, HEADS, N], BF16) for i in range(STACK_RING)]
                v_sb = [sb(f"v{i}", [P, TT, HEADS, VW]) for i in range(V_RING)]
                probs = [sb(f"probs{i}", [P, TT * N]) for i in range(P_RING)]
                neg_hi = sb("neg_max_hi", [HEADS * TT, P], BF16)
                neg_lo = sb("neg_max_lo", [HEADS * TT, P], BF16)
                gate = sb("gate", [P, C])
                o_t = [sb(f"o_transposed{i}", [P, GROUPS * N]) for i in range(2)]
                recip_b = sb("reciprocals", [P, GROUPS * N])
                sums = sb("row_sums", [P, PV_HEADS * GROUPS * N // P])
                recip = sb("row_reciprocals", [P, PV_HEADS * GROUPS * N // P])
                gated = sb("gated", [P, C])

                w_ok = prepared["attn_weights", l]
                k_ones = {}
                v_one = []
                pv = psum[4]

                if l == 0:
                    act.queue.append(lambda q: q.preload_act_table_set("natural_log_exp_and_others"))
                parts_free = [None] * PARTS_RING
                rest_free, z_free = [None, None], [None] * Z_RING
                part_marks = {}
                stack_ok, v_ok = {}, {}
                scratch_free = [None, None]
                last_scores = {}
                max_ok, max_t_ok, exp_ok, pv_done, neg_ok = {}, {}, {}, {}, {}
                smax_free, st_free = [None, None], [None, None]
                probs_free = [None] * P_RING
                sq_free, rstd_free = [None, None], [None, None]
                state = {"gate_free": None, "neg": None,
                         "sums": None, "recip": None, "recip_b": None, "gated": None}
                o_free = [None, None]
                v_free = [None] * V_RING

                def load_mod(b):
                    return sp.dma(mod[:], mod_d[l, b:b + 1, 0:2 * C].broadcast_to([P, 2 * C]), s_mod, ln.mod_read,
                                  prepared["mod", l])

                chunks_done = [0]

                def qk_chunk(b, m, xt, xt_ok):
                    c0, rows = QK_CHUNKS[m]
                    slot = HEADS * b + CHUNK_SLOTS[m]
                    bank = take()
                    mm = matmuls(wide_steps(bank.ap[0:rows, 0:N], w_attn, xt, (c0, c0 + rows), (0, N), True),
                                 xt_ok, w_ok, bank.free)
                    n = chunks_done[0]
                    chunks_done[0] += 1
                    i, pi, zi = n % 2, n % PARTS_RING, n % Z_RING
                    a_part, b_part, c_part = (parts[pi][0:rows, j, :] for j in range(3))
                    r = rest[i][0:rows, :]
                    yield slot + 1
                    if l == 1:
                        ak = copy(act, a_part, bank.ap[0:rows, 0:N], mm, parts_free[pi])
                        yield slot + 2
                        rk = put(bank, tt(dve, r, bank.ap[0:rows, 0:N], a_part, ALU.subtract, ak, rest_free[i]))
                        yield slot + 3
                        bk = copy(act, b_part, r, rk, parts_free[pi])
                        yield slot + 4
                    else:
                        z, sq, qk_rstd = z_sb[zi][0:rows, :], sq_sb[i][0:rows, :], rstd_sb[i][0:rows, :]
                        zk = put(bank, copy(act, z, bank.ap[0:rows, 0:N], mm, z_free[zi]))
                        sk = func(sq, z, ACT.Square, zk, sq_free[i])
                        yield slot + 2
                        bank = take()
                        vk = sq_free[i] = pe.do(lambda q: q.matmul(bank.ap[0:rows, 0:N], head_ones[0:rows, 0:rows],
                                                                   sq, start=True, stop=True),
                                                sk, bank.free, head_ones_ok)
                        yield slot + 3
                        lk = put(bank, func(qk_rstd, bank.ap[0:rows, 0:N], ACT.Ln, vk, rstd_free[i], const_ok,
                                            bias=eps_col[0:rows, :], scale=1.0 / HD))
                        ek = func(qk_rstd, qk_rstd, ACT.Exp, lk, scale=-0.5)
                        yield slot + 4
                        yk = rstd_free[i] = stt(z, z, qk_gain[0:rows, m:m + 1], qk_rstd, ALU.mult, ALU.mult, ek, zk)
                        yield slot + 5
                        ak = copy(act, a_part, z, yk, parts_free[pi])
                        yield slot + 6
                        rk = z_free[zi] = tt(dve, r, z, a_part, ALU.subtract, ak, rest_free[i])
                        bk = copy(dve, b_part, r, rk, parts_free[pi])
                        yield slot + 7
                    ck = rest_free[i] = tt(pool, c_part, r, b_part, ALU.subtract, bk)
                    dst = parts_d[b % 2][:, c0:c0 + rows, :].rearrange("j r n -> r j n")
                    part_marks[b, m] = parts_free[pi] = sp.dma(dst, parts[pi][0:rows, :, :], s_parts[m], ck, scratch_free[b % 2])

                def load_stacks(b):
                    ring, d = b % STACK_RING, parts_d[b % 2]
                    after = [part_marks[b, m] for m in range(len(QK_CHUNKS))] + [last_scores.get(b - STACK_RING), k_ones[ring]]
                    for j, (qp, kp) in enumerate(((0, 0), (0, 1), (0, 2), (1, 0), (1, 1), (2, 0))):
                        for st, p, c0 in ((q_st, qp, 0), (k_st, kp, C)):
                            mark = sp.dma(st[ring][HD * j:HD * j + HD, :, :],
                                          d[p, c0:c0 + C, :].rearrange("(h r) n -> r h n", r=HD), s_stack[ring], after)
                    stack_ok[b] = scratch_free[b % 2] = mark


                def value_tile(b, t, xt, xt_ok):
                    bank = take()
                    mm = matmuls(wide_steps(bank.ap[:, 0:C], w_attn, xt, (QK, 3 * C), (t * P, t * P + P), False),
                                 xt_ok, w_ok, bank.free)
                    ln.xt_free = [mm]
                    yield HEADS * b + VALUE_SLOTS[t] + 1
                    vk = copy(dve, v_sb[b % V_RING][:, t, :, 0:HD], bank.ap[:, 0:C].rearrange("p (h d) -> p h d", d=HD),
                              mm, v_free[b % V_RING], v_one)
                    v_ok.setdefault(b, []).append(put(bank, vk))

                def front(b):
                    mod_ok = load_mod(b)
                    start = HEADS * b + FRONT_START
                    yield start + 3
                    yield from ln.run(b, start + 3, start + 18, mod[:, 0:C], mod[:, C:2 * C], mod_ok, take, put)
                    xt, xt_ok = ln.ready
                    for m, slot in enumerate(CHUNK_SLOTS):
                        yield HEADS * b + slot
                        yield qk_chunk(b, m, xt, xt_ok)
                    for t, slot in enumerate(VALUE_SLOTS):
                        yield HEADS * b + slot
                        yield value_tile(b, t, xt, xt_ok)
                    yield HEADS * b + STACKS_SLOT
                    load_stacks(b)

                def place_maxima(b):
                    slot = HEADS * b - MAX_LEAD + HEADS + 1
                    yield slot + 1
                    bank = take()
                    rows = HEADS * TT
                    tr = max_t_ok[b] = pe.do(
                        lambda q: q.transpose(bank.ap[0:rows, 0:P], maxes[b % 2][:].rearrange("p h t -> p (h t)"), ident),
                        max_ok[b, HEADS - 1], bank.free, ident_ok)
                    yield slot + 2
                    hk = dve.do(lambda q: q.tensor_scalar(neg_hi[:], bank.ap[0:rows, 0:P], -1.0, None, ALU.mult), tr, state["neg"])
                    lk = put(bank, stt(neg_lo[:], bank.ap[0:rows, 0:P], -1.0, neg_hi[:], ALU.mult, ALU.subtract, hk))
                    yield slot + 3
                    for src, row in ((neg_hi, STACK), (neg_lo, STACK + 1)):
                        dst = q_st[b % STACK_RING][row:row + 1, :, :].rearrange("o h (t n) -> o (h t) n", t=TT)
                        neg_ok[b] = state["neg"] = sp.dma(dst, src[:], s_max, lk, last_scores.get(b - STACK_RING))

                def max_scores(b, h):
                    ring, i = b % STACK_RING, h % 2
                    bank = psum[i]
                    qs, ks = q_st[ring], k_st[ring]

                    def emit(q):
                        for t in range(TT):
                            last = q.matmul(bank.ap[:, t * N:t * N + N], qs[0:STACK, h, t * P:t * P + P], ks[0:STACK, h, :],
                                            start=True, stop=True)
                        return last
                    return pe.do(emit, stack_ok[b], smax_free[i])

                def reduce_max(b, h, mm):
                    i = h % 2
                    max_ok[b, h] = smax_free[i] = dve.do(
                        lambda q: q.tensor_reduce(maxes[b % 2][:, h, :], psum[i].ap[:].rearrange("p (t n) -> p t n", t=TT), AX.X, ALU.max),
                        mm, max_t_ok.get(b - 2))

                def shifted_scores(b, h):
                    ring, i = b % STACK_RING, h % 2
                    bank = psum[2 + i]
                    qs, ks = q_st[ring], k_st[ring]

                    def emit(q):
                        for t in range(TT):
                            last = q.matmul(bank.ap[:, t * N:t * N + N], ks[0:STACK + 2, h, t * P:t * P + P],
                                            qs[0:STACK + 2, h, :], start=True, stop=True)
                        return last
                    mm = pe.do(emit, stack_ok[b], neg_ok[b], st_free[i])
                    last_scores[b] = mm
                    return mm

                def exponentials(b, h, mm):
                    i = h % 2
                    r = (b * HEADS + h) % P_RING
                    exp_ok[b, h] = st_free[i] = func(probs[r][:], psum[2 + i].ap[:], ACT.Exp, mm, probs_free[r], scale=SCORE_SCALE)

                def weigh_values(b, g):
                    def emit(q):
                        for t in range(TT):
                            for i in range(PV_HEADS):
                                h = g * PV_HEADS + i
                                r = (b * HEADS + h) % P_RING
                                last = q.matmul(pv.ap[32 * i:32 * i + VW, 0:N], v_sb[b % V_RING][:, t, h, :],
                                                probs[r][:, t * N:t * N + N], start=(t == 0), stop=(t == TT - 1))
                        return last
                    mm = pe.do(emit, v_ok[b], [exp_ok[b, g * PV_HEADS + i] for i in range(PV_HEADS)], pv.free)
                    for i in range(PV_HEADS):
                        probs_free[(b * HEADS + g * PV_HEADS + i) % P_RING] = mm
                    v_free[b % V_RING] = mm
                    return mm

                def values(b, g, slot):
                    mm = weigh_values(b, g)
                    yield slot + 1
                    pv_done[b, g] = pv.free = copy(act, o_t[b % 2][:, g * N:g * N + N], pv.ap[:, 0:N], mm, o_free[b % 2])

                    if g == GROUPS - 1:
                        yield back(b)

                def back(b):
                    first = HEADS * b + HEADS + 2
                    o = o_t[b % 2]
                    yield first + 1
                    k = sp.dma(sums[:], o[HD:HD + 97:32, :].rearrange("i (q n) -> i q n", n=sums.shape[1]), s_sums,
                               pv_done[b, GROUPS - 1], state["recip"])
                    yield first + 4
                    rk = dve.do(lambda q: q.reciprocal(recip[:], sums[:]), k, state["recip"])
                    yield first + 5
                    state["recip"] = k = sp.dma(recip_d.rearrange("i (q n) -> (i q) n", n=sums.shape[1]), recip[:], s_recip, rk,
                                                state["recip_b"])
                    yield first + 7
                    bk = sp.dma(recip_b[:], recip_d.rearrange("i (o n) -> i o n", o=1).broadcast_to([PV_HEADS, 32, GROUPS * N]),
                                s_recip_in, k, state["recip_b"])
                    gate_ok = sp.dma(gate[:], mod_d[l, b:b + 1, 2 * C:3 * C].broadcast_to([P, C]), s_gate, state["gate_free"],
                                     prepared["mod", l])
                    yield first + 11
                    half = GROUPS * N // 2
                    nk = []
                    for j, engine in enumerate((dve, pool)):
                        cols = slice(half * j, half * j + half)
                        nk.append(tt(engine, o[:, cols], o[:, cols], recip_b[:, cols], ALU.mult, bk))
                    state["recip_b"] = nk
                    for t, (slot, second) in enumerate(PROJ_SLOTS):
                        yield HEADS * b + slot
                        bank = take()

                        def project(groups, t=t, bank=bank):
                            def emit(q):
                                for g in groups:
                                    last = q.matmul(bank.ap[:, 0:C], o[:, g * N + t * P:g * N + t * P + P], w_proj[:, g, :],
                                                    start=(g == 0), stop=(g == GROUPS - 1))
                                return last
                            return pe.do(emit, nk, w_ok, bank.free)

                        project(range(GROUPS // 2))
                        yield HEADS * b + second
                        mm = project(range(GROUPS // 2, GROUPS))
                        yield gate_and_add(b, t, bank, mm, HEADS * b + second, gate_ok)
                    o_free[b % 2] = mm

                def gate_and_add(b, t, bank, mm, slot, gate_ok):
                    yield slot + 1
                    gk = state["gate_free"] = put(bank, tt(dve, gated[:], bank.ap[:, 0:C], gate[:], ALU.mult, mm, gate_ok,
                                                           state["gated"]))
                    yield slot + 2
                    xt = x_sb[:, TT * b + t, :]
                    x_marks[TT * b + t] = state["gated"] = tt(pool, xt, xt, gated[:], ALU.add, gk)

                agenda = Agenda(FRONT_START)
                maxima = exps = None
                for T in range(FRONT_START, HEADS * B + 3):
                    b, h = divmod(T, HEADS)
                    if rest_before:
                        rest_before = rest_before()
                    if T == FRONT_START + REST_SLOTS:
                        assert not rest_before
                        meet()
                        for t in v_sb:
                            dve.do(lambda q, t=t: q.memset(t[:, :, :, HD:HD + 1], 1.0))
                            v_one.append(dve.do(lambda q, t=t: q.memset(t[:, :, :, HD + 1:VW], 0.0)))
                        pv.free = dve.do(lambda q: q.memset(pv.ap[:, 0:N], 0.0))
                    if T - HEADS * B in FC1_LOAD_SLOTS:
                        g = FC1_LOAD_SLOTS.index(T - HEADS * B)
                        if g == 0:
                            meet(sp)
                        w1_here[l][1].append(load_stacked(w1, fc1_d[l][g], slice(group * g, group * (g + 1)), s_w_fc1[g],
                                                          prepared["fc1", l]))
                    if T - FRONT_START in ONES_SLOTS:
                        i = ONES_SLOTS.index(T - FRONT_START)
                        k_ones[i] = pool.do(lambda q, i=i: q.memset(k_st[i][96:128, :, :], 1.0), (pool.sem, pool.count))
                        pool.wait(k_ones[i])
                    if deferred and (T == -HEADS * 4 or T > 0 and T % 4 == 0):
                        call, *args = deferred.pop(0)
                        call(*args)
                    if exps:
                        exponentials(*exps)
                    if maxima:
                        reduce_max(*maxima)
                        if maxima[1] == HEADS - 1:
                            agenda.start(place_maxima(maxima[0]))
                    mb, mh = divmod(T + MAX_LEAD, HEADS)
                    maxima = (mb, mh, max_scores(mb, mh)) if 0 <= mb < B else None
                    exps = (b, h, shifted_scores(b, h)) if 0 <= b < B else None
                    fb, fh = divmod(T - FRONT_START, HEADS)
                    if fh == 0 and fb < B:
                        agenda.start(front(fb), last=True)
                    agenda.run(T)
                    vb, vh = divmod(T - 2, HEADS)
                    if 0 <= vb < B and vh % PV_HEADS == PV_HEADS - 1:
                        agenda.start(values(vb, vh // PV_HEADS, T))
                meet()
                return rest_of(agenda, HEADS * B + 3)
            return run

        CHUNKS = MLP // P
        SLOTS = CHUNKS + 6

        def mlp(l):
            def run(sb, rest_before):
                banks = Banks(psum[:8 - PSUM_RING])
                take, put = banks.take, banks.put

                sb("room_of_w_fc1", [P, WIDE_CHUNKS * MLP])
                w1, w1_loaded = w1_here[l]
                w2 = {part: sb(f"w_fc2_{part}", [P, CHUNKS, C], F32R) for part in ("hi", "lo")}
                ln = Normaliser(sb, 2)
                mod = [sb(f"scale_shift{i}", [P, 2 * C]) for i in range(2)]
                gate = [sb(f"gate_and_gated_bias{i}", [P, 2 * C]) for i in range(2)]
                hidden = [sb(f"hidden{i}", [P, N]) for i in range(3)]
                gated = [sb(f"gated{i}", [P, C]) for i in range(TT)]
                h_hi, h_lo = [], []
                for i in range(2):
                    h_hi.append(sb(f"hidden_hi{i}", [P, CHUNKS, N], F32R))
                    h_lo.append(sb(f"hidden_lo{i}", [P, CHUNKS, N], F32R))
                mod_free, gate_free, h_free, gated_free = [None] * 2, [None] * 2, [None] * 2, [None] * TT
                hidden_free = [None] * 3
                chunks_done = [0]
                w1_ok, w2_ok, h_split = {}, [], {}
                scratch_w = w2["hi"][:].rearrange("p c n -> p (c n)")

                def front(b):
                    i, start = b % 2, SLOTS * b - SLOTS
                    mod_ok = sp.dma(mod[i][:], mod_d[l, b:b + 1, 3 * C:5 * C].broadcast_to([P, 2 * C]), s_mod2[i], mod_free[i],
                                    prepared["mod", l])
                    yield start + 2
                    yield from ln.run(b, start + 2, start + 10, mod[i][:, 0:C], mod[i][:, C:2 * C], mod_ok, take, put)
                    mod_free[i] = ln.mod_read

                def fc1(b):
                    i, start = b % 2, SLOTS * b
                    xt, xt_ok = ln.ready
                    h_split[b] = []
                    for m in range(CHUNKS):
                        yield start + m
                        bank = take()
                        mm = matmuls(wide_steps(bank.ap[:, 0:N], w1, xt, (m * P, m * P + P), (0, N), True), xt_ok,
                                     w1_ok[m * P // group], bank.free)
                        yield activate(b, m, bank, mm, start + m)
                    ln.xt_free[i] = mm

                def activate(b, m, bank, mm, slot):
                    i, r = b % 2, chunks_done[0] % 3
                    chunks_done[0] += 1
                    yield slot + 1
                    gk = put(bank, func(hidden[r][:], bank.ap[:, 0:N], ACT.Gelu_apprx_tanh, mm, hidden_free[r]))
                    yield slot + 2
                    after = [h_free[i], h_ready]
                    hk = copy(dve, h_hi[i][:, m, :], hidden[r][:], gk, after)
                    lk = hidden_free[r] = tt(dve, h_lo[i][:, m, :], hidden[r][:], fp(h_hi[i][:, m, :]), ALU.subtract, hk, after)
                    h_split[b] += [hk, lk]

                def fc2(b):
                    i, start = b % 2, SLOTS * b + SLOTS + CHUNKS
                    yield start - 5
                    gate_ok[b] = sp.dma(gate[i][:], mod_d[l, b:b + 1, 5 * C:7 * C].broadcast_to([P, 2 * C]), s_gate2[i],
                                        gate_free[i], prepared["mod", l])
                    yield start
                    for t in range(TT):
                        bank = take()
                        cols = slice(t * P, t * P + P)
                        for third in range(3):
                            yield start + 3 * t + third

                            def emit(q, bank=bank, cols=cols, third=third):
                                for c in range(3 * third, 3 * third + 3):
                                    for x, w in ((h_hi, "hi"), (h_hi, "lo"), (h_lo, "hi")):
                                        last = q.matmul(bank.ap[:, 0:C], x[i][:, c, cols], w2[w][:, c, :],
                                                        start=(c == 0 and x is h_hi and w == "hi"),
                                                        stop=(c == CHUNKS - 1 and x is h_lo))
                                return last
                            mm = pe.do(emit, h_split[b], w2_ok, bank.free)
                        yield gate_and_add(b, t, bank, mm, start + 3 * t + 2)
                    h_free[i] = mm

                def gate_and_add(b, t, bank, mm, slot):
                    i = b % 2
                    yield slot + 1
                    gk = put(bank, tt(dve, gated[t][:], bank.ap[:, 0:C], gate[i][:, 0:C], ALU.mult, mm, gate_ok[b], gated_free[t]))
                    yield slot + 2
                    xt = x_sb[:, TT * b + t, :]
                    k = gated_free[t] = tt(pool, xt, xt, gated[t][:], ALU.add, gk)
                    k = x_marks[TT * b + t] = gate_free[i] = tt(pool, xt, xt, gate[i][:, C:2 * C], ALU.add, k)
                    if t == TT - 1 and l == LAYERS - 1:
                        yield slot + 4
                        sp.dma(out[b].rearrange("(t p) c -> p t c", p=P), x_sb[:, TT * b:TT * b + TT, :], s_out, k)

                gate_ok = {}
                h_ready = None
                agenda = Agenda(-SLOTS)
                last = l == LAYERS - 1
                for T in range(-SLOTS, SLOTS * (B + 1) + 6 if last else SLOTS * B + 4):
                    b, s = divmod(T, SLOTS)
                    if rest_before:
                        rest_before = rest_before()
                        if not rest_before:
                            h_ready = [(e.sem, e.count) for e in (pe, dve, pool)] + [(s_gate.sem, s_gate.count)]
                            banks.idle += psum[8 - PSUM_RING:]
                    if T in FC1_SPLIT_SLOTS:
                        g = FC1_SPLIT_SLOTS.index(T)
                        w1_ok[g] = split_stacked(w1, w1, slice(group * g, group * (g + 1)), scratch_w[:, group * g:group * (g + 1)],
                                                 w1_loaded[g])
                    if T == FC2_LOAD_SLOT:
                        w2_raw = sp.dma(fp(w2["lo"][:]), fc2_d[l], s_w_fc2, prepared["fc2", l])
                    if s == 0:
                        if b + 1 < B:
                            agenda.start(front(b + 1))
                        if 0 <= b < B:
                            agenda.start(fc1(b))
                            agenda.start(fc2(b))
                        if b == 2 and not last:
                            raw_ok = load_stacked(w_attn, qkv_d, slice(0, 3 * C), s_w, prepared["qkv", 1])
                        if b == 4 and not last:
                            split_ok = split_stacked(w_attn, w_attn, slice(0, 3 * C), proj_space, raw_ok)
                            prepared["attn_weights", l + 1] = split_ok + load_proj(l + 1, split_ok)
                    if T == CHUNKS:
                        w2_ok.append(copy(act, w2["hi"][:], fp(w2["lo"][:]), w2_raw, [w1_ok[g] for g in w1_ok]))
                        w2_ok.append(tt(dve, w2["lo"][:], fp(w2["lo"][:]), fp(w2["hi"][:]), ALU.subtract, w2_ok[0]))
                    agenda.run(T)
                meet()
                if last:
                    return None
                assert len(banks.idle) == 8
                banks.idle = [bk for bk in banks.idle if bk in psum[:8 - PSUM_RING]]
                return rest_of(agenda, SLOTS * B + 4)
            return run

        phase("prep", prepare)
        meet()
        rest = None
        for l in range(LAYERS):
            rest = phase(f"attn{l}", attention(l), rest)
            rest = phase(f"mlp{l}", mlp(l), rest)

        block = outer.enter_context(nc.Block())
        block.tensor(pe.play)
        block.scalar(act.play)
        block.vector(dve.play)
        block.gpsimd(pool.play)
        block.sync(sp.play)


_INS = ['x', 'cond_1152', 'L0_cond_w_mod', 'L0_cond_b_mod', 'L0_cond_w_qkv', 'L0_cond_b_qkv', 'L0_cond_g_q', 'L0_cond_g_k',
        'L0_cond_w_proj', 'L0_cond_b_proj', 'L0_cond_w1', 'L0_cond_b1', 'L0_cond_w2', 'L0_cond_b2',
        'L1_cond_W_qkv', 'L1_cond_b_qkv', 'L1_cond_W_proj', 'L1_cond_b_proj', 'L1_cond_W_fc1', 'L1_cond_b_fc1',
        'L1_cond_W_fc2', 'L1_cond_b_fc2', 'L1_cond_W_ada', 'L1_cond_b_ada']


def kernel(**inputs):
    import numpy as _np
    import concourse.bacc as _bacc
    from concourse import mybir as _mybir
    from concourse.bass_utils import run_bass_kernel_spmd as _run

    nc = _bacc.Bacc("TRN2", target_bir_lowering=False, num_devices=1, dynamic_dma_scratch_size=64)
    arrays, aps = {}, {}
    for name in _INS:
        v = _np.ascontiguousarray(inputs[name])
        arrays[f"in_{name}_dram"] = v
        aps[name] = nc.dram_tensor(f"in_{name}_dram", v.shape, _mybir.dt.from_np(v.dtype), kind="ExternalInput").ap()
    out = nc.dram_tensor("out_0_dram", (B, N, C), F32, kind="ExternalOutput").ap()
    build(nc, aps, out)
    r = _run(nc, [arrays], core_ids=[0])
    return r.results[0]["out_0_dram"]
```

```python
from contextlib import ExitStack

import concourse.bass as bass
from concourse import mybir

F32 = mybir.dt.float32
F32R = mybir.dt.float32r
BF16 = mybir.dt.bfloat16
ALU = mybir.AluOpType
ACT = mybir.ActivationFunctionType
AX = mybir.AxisListType

B, N, C = 32, 256, 288
HEADS = 16
HD = C // HEADS
MLP = 4 * C
FC1_LOADS = 3
LAYERS = 2
MLP_WEIGHTS = (("L0_cond_w1", "L0_cond_b1", "L0_cond_w2"), ("L1_cond_W_fc1", "L1_cond_b_fc1", "L1_cond_W_fc2"))
X_LOADS = 16
P = 128
TT = N // P
EPS = 1e-6
SCORE_SCALE = float(HD) ** -0.5
K3 = C // 3

XS_COLS = 2 * C + 32
WIDE_ROWS = [128, 128, 128, 128, 98]
WIDE_CHUNKS = 7
WIDE_PAIRS = [(0, 0), (1, 1), (2, 2), (3, 3), (4, 4), (5, 0), (6, 1)]

QK = 2 * C
QK_M = 7 * HD
QK_CHUNKS = [(m, min(QK_M, QK - m)) for m in range(0, QK, QK_M)]
STACK = 6 * HD
VW = HD + 2
PV_HEADS = 4
GROUPS = HEADS // PV_HEADS

STACK_RING, V_RING, P_RING, PSUM_RING = 3, 5, 6, 3
Z_RING, PARTS_RING = 4, 4

MAX_LEAD = HEADS + 8
REST_SLOTS = 16
LEFT_SLOT, MLP_FRONT_SLOT = -26, -15
FC1_LOAD_SLOTS = [-12, -6, -2]
FC1_SPLIT_SLOTS = [-7, -1]
MLP_FIRST_SLOT = -5
FC2_LOAD_SLOT, FC2_SPLIT_SLOT = -2, 19
DEFERRED_START, DEFERRED_SLOTS = -64, (14, 15, 0)
FRONT_START = -79
CHUNK_SLOTS = [-57, -56, -54, -53, -52]
VALUE_SLOTS = [-50, -49]
STACKS_SLOT = -32
PROJ_SLOTS = [(32, 34), (36, 37)]


class Engine:

    def __init__(self, sem):
        self.sem, self.count, self.queue, self.seen = sem, 0, [], {}

    def wait(self, *after):
        for mark in flat(after):
            sem, value = mark
            if self.seen.get(id(sem), 0) < value:
                self.seen[id(sem)] = value
                self.queue.append(lambda e, s=sem, v=value: e.wait_ge(s, v))

    def do(self, emit, *after):
        self.wait(*after)
        self.count += 1
        self.queue.append(lambda e, f=emit: f(e).then_inc(self.sem, 1))
        return (self.sem, self.count)

    def dma(self, out, in_, stream, *after):
        self.wait(*after)
        stream.count += 16
        self.queue.append(lambda e, s=stream.sem: e.dma_start(out, in_).then_inc(s, 16))
        return (stream.sem, stream.count)

    def play(self, e):
        for step in self.queue:
            step(e)


class Stream:

    def __init__(self, sem):
        self.sem, self.count = sem, 0


def flat(marks):
    for m in marks:
        if m is None:
            continue
        if isinstance(m, list):
            yield from flat(m)
        else:
            yield m


class Bank:

    def __init__(self, ap):
        self.ap, self.free = ap, None


class Banks:

    def __init__(self, banks):
        self.idle = list(banks)

    def take(self):
        return self.idle.pop(0)

    def put(self, bank, mark):
        bank.free = mark
        self.idle.append(bank)
        return mark


class Agenda:

    def __init__(self, slot):
        self.slot, self.started, self.waiting = slot, 0, []

    def start(self, g, last=False):
        self.started += 1
        self.step((last, self.started), g)

    def step(self, age, g):
        for then in g:
            if isinstance(then, int):
                if then > self.slot:
                    self.waiting.append((age, then, g))
                    return
            else:
                self.start(then)

    def run(self, slot):
        self.slot = slot
        due = sorted((w for w in self.waiting if w[1] <= slot), key=lambda w: w[0])
        self.waiting = [w for w in self.waiting if w[1] > slot]
        for age, _, g in due:
            self.step(age, g)


def build(nc, a, out):
    outer = ExitStack()
    with outer:
        def sem(name):
            return outer.enter_context(nc.semaphore(name))

        def stream(name):
            return Stream(sem(name))

        pe, act, dve, pool, sp = (Engine(sem(n)) for n in ("pe_done", "act_done", "dve_done", "pool_done", "sp_unused"))
        engines = [pe, act, dve, pool, sp]

        def sb_in(scope, name, shape, dt=F32):
            return scope.enter_context(nc.sbuf_tensor(name, shape, dt))

        def phase(name, build_phase, *before):
            with ExitStack() as scope:
                return build_phase(lambda n, shape, dt=F32: sb_in(scope, f"{name}_{n}", shape, dt), *before)

        def all_so_far():
            return [(s.sem, s.count) for s in engines + streams if s.count]

        def meet(*who):
            marks = all_so_far()
            for e in who or engines:
                e.wait(marks)

        def rest_of(agenda, slot):
            def step():
                nonlocal slot
                agenda.run(slot)
                slot += 1
                return step if agenda.waiting else None
            return step

        streams = []

        def new_stream(name):
            s = stream(name)
            streams.append(s)
            return s

        x_sb = sb_in(outer, "x_resident", [P, B * TT, C])
        ident_wide = sb_in(outer, "identity_between_zeros", [P, 3 * P], F32R)
        ident = ident_wide[:, P:2 * P].bitcast(F32)
        head_ones = sb_in(outer, "head_block_ones", [P, P])
        minus_half = sb_in(outer, "minus_half", [P, TT])
        minus_lo_row = sb_in(outer, "minus_one_on_low_rows", [P, 1])
        eps_col = sb_in(outer, "eps_column", [P, 1])
        qk_gain = sb_in(outer, "qk_gain", [P, len(QK_CHUNKS)])
        w_attn = sb_in(outer, "w_qkv_stacked", [P, WIDE_CHUNKS, 3 * C], F32R)
        w_proj = sb_in(outer, "w_proj_by_heads", [P, GROUPS, C])
        psum = [Bank(outer.enter_context(nc.psum_tensor(f"psum{i}", [P, 512], F32))) for i in range(8)]

        def scratch(name, shape, dt=F32):
            return nc.dram_tensor(name, shape, dt).ap()

        mod_d = scratch("modulation", (LAYERS, B, 7 * C))
        group = MLP // FC1_LOADS
        qkv_d = scratch("qkv_stacked", (P, WIDE_CHUNKS, 3 * C))
        fc1_d = [[scratch(f"fc1_stacked_{l}_{g}", (P, WIDE_CHUNKS, group)) for g in range(FC1_LOADS)] for l in range(LAYERS)]
        fc2_d = [scratch(f"fc2_by_rows_{l}", (P, MLP // P, C)) for l in range(LAYERS)]
        parts_d = [scratch(f"qk_parts_{i}", (3, QK, N), BF16) for i in range(2)]
        ones_d = scratch("ones", (2, HEADS, N), BF16)
        recip_d = scratch("row_reciprocals", (PV_HEADS, GROUPS * N))

        s_x = [stream(f"x_loaded_{i}") for i in range(X_LOADS)]
        s_out = new_stream("out_stored")
        s_ones_out = new_stream("ones_stored")
        s_ones = new_stream("ones_placed")
        s_gain = new_stream("gains_loaded")
        s_cond = new_stream("cond_loaded")
        s_w_mod = [new_stream(f"w_mod_loaded_{l}") for l in range(LAYERS)]
        s_mod_rows = [new_stream(f"mod_rows_stored_{l}") for l in range(LAYERS)]
        s_w = new_stream("attn_weights_loaded")
        s_w_proj = stream("proj_weights_loaded")
        s_w_fc1 = [new_stream(f"fc1_weights_loaded_{i}") for i in range(FC1_LOADS)]
        s_w_fc2 = new_stream("fc2_weights_loaded")
        s_order_fc1 = [stream(f"fc1_arranged_{l}") for l in range(LAYERS)]
        s_order_fc2 = [stream(f"fc2_arranged_{l}") for l in range(LAYERS)]
        s_order_qkv = stream("qkv_arranged")
        s_mod = new_stream("attn_mod_loaded")
        s_gate = new_stream("attn_gate_loaded")
        s_mod2 = [new_stream(f"mlp_mod_loaded_{i}") for i in range(2)]
        s_gate2 = [new_stream(f"mlp_gate_loaded_{i}") for i in range(2)]
        s_parts = [new_stream(f"parts_stored_{m}") for m in range(len(QK_CHUNKS))]
        s_stack = [new_stream(f"stack_loaded_{i}") for i in range(STACK_RING)]
        s_max = new_stream("maxima_placed")
        s_sums = new_stream("sums_spread")
        s_recip = new_stream("reciprocals_stored")
        s_recip_in = new_stream("reciprocals_loaded")

        def copy(e, out_, in_, *after):
            if e is act:
                return e.do(lambda q: q.activation(out_, in_, ACT.Copy), *after)
            return e.do(lambda q: q.tensor_copy(out_, in_), *after)

        def tt(e, out_, in0, in1, op, *after):
            return e.do(lambda q: q.tensor_tensor(out_, in0, in1, op), *after)

        def stt(out_, in0, scalar, in1, op0, op1, *after):
            return dve.do(lambda q: q.scalar_tensor_tensor(out=out_, in0=in0, scalar=scalar, in1=in1, op0=op0, op1=op1), *after)

        def func(out_, in_, f, *after, **kw):
            return act.do(lambda q: q.activation(out_, in_, f, **kw), *after)

        def matmuls(steps, *after):
            def emit(q):
                last = None
                for i, (o, l, r) in enumerate(steps):
                    last = q.matmul(o, l, r, start=(i == 0), stop=(i == len(steps) - 1))
                return last
            return pe.do(emit, *after)

        def fp(ap):
            return ap.bitcast(F32)

        def wide_steps(out_, weights, acts, w_cols, a_cols, weights_stationary):
            steps = []
            for kw, ka in WIDE_PAIRS:
                rows = WIDE_ROWS[ka]
                w = weights[0:rows, kw, w_cols[0]:w_cols[1]]
                x = acts[0:rows, ka, a_cols[0]:a_cols[1]]
                steps.append((out_, w, x) if weights_stationary else (out_, x, w))
            return steps

        draft = w_proj[:].rearrange("p g n -> p (g n)")[:, 0:3 * P]
        k = dve.do(lambda q: q.memset(draft, 0.0))
        k = pool.do(lambda q: q.affine_select(out=draft, in_=draft, compare_op=ALU.not_equal, fill=1.0,
                                              base=P, pattern=[[-1, 3 * P]], channel_multiplier=1), k)
        ident_ok = copy(dve, ident_wide[:], draft, k)
        k = dve.do(lambda q: q.memset(head_ones[:], 1.0))
        blocks = head_ones[:, 0:QK_M].rearrange("p (j d) -> p j d", d=HD)
        k = pool.do(lambda q: q.affine_select(out=blocks, in_=blocks, compare_op=ALU.is_ge, fill=0.0,
                                              base=0, pattern=[[-HD, 7], [0, HD]], channel_multiplier=1), k)
        head_ones_ok = pool.do(lambda q: q.affine_select(out=blocks, in_=blocks, compare_op=ALU.is_ge, fill=0.0,
                                                         base=HD - 1, pattern=[[HD, 7], [0, HD]], channel_multiplier=-1), k)
        dve.do(lambda q: q.memset(eps_col[:], EPS))
        k = dve.do(lambda q: q.memset(minus_lo_row[:], -1.0))
        k = dve.do(lambda q: q.memset(minus_lo_row[0:64, :], 0.0), k)
        dve.do(lambda q: q.memset(minus_lo_row[96:97, :], 0.0), k)
        dve.do(lambda q: q.memset(minus_half[:], -0.5))
        const_ok = (dve.sem, dve.count)

        gk_col = sb_in(outer, "g_k_columns", [P, len(QK_CHUNKS)])
        dve.do(lambda q: q.memset(qk_gain[:], 1.0))
        const_gain = dve.do(lambda q: q.memset(gk_col[:], 1.0))

        prepared, x_marks = {}, {}

        def prepare(sb):
            ones = sb("ones", [2, HEADS, N], BF16)
            ones_ok = dve.do(lambda q: q.memset(ones[:], 1.0))
            cond = sb("cond", [B, C])
            silu_a = sb("silu_denominator", [B, C])
            silu_b = sb("silu", [B, C])
            silu_t = sb("silu_transposed", [K3, 3, B])
            loaded = sp.dma(cond[:], a["cond_1152"], s_cond)
            k = func(silu_a[:], cond[:], ACT.Exp, loaded, scale=-1.0)
            k = dve.do(lambda q: q.tensor_scalar(silu_a[:], silu_a[:], 1.0, None, ALU.add), k)
            k = dve.do(lambda q: q.reciprocal(silu_a[:], silu_a[:]), k)
            silu_ok = tt(dve, silu_b[:], cond[:], silu_a[:], ALU.mult, k)
            for i in range(3):
                t = pe.do(lambda q, i=i: q.transpose(psum[i].ap[0:K3, 0:B], silu_b[:, K3 * i:K3 * i + K3], ident[0:B, 0:B]),
                          silu_ok, ident_ok)
                silu_t_ok = psum[i].free = copy(dve, silu_t[:, i, :], psum[i].ap[0:K3, 0:B], t)
            w_mod = [sb(f"w_mod{l}", [K3, 3, 6 * C]) for l in range(LAYERS)]
            b_mod = [sb(f"b_mod{l}", [B, 6 * C]) for l in range(LAYERS)]
            b_2 = [sb(f"b_fc2_{l}", [B, C]) for l in range(LAYERS)]
            rows = [sb(f"mod_rows{l}", [B, 7 * C]) for l in range(LAYERS)]
            order = [1, 0, 2, 4, 3, 5]
            names = (("L0_cond_w_mod", "L0_cond_b_mod", "L0_cond_b2"), ("L1_cond_W_ada", "L1_cond_b_ada", "L1_cond_b_fc2"))

            def load_modulation(l):
                w, bias, b2 = names[l]
                sp.dma(w_mod[l][:], a[w].rearrange("(i p) n -> p i n", p=K3), s_w_mod[l])
                sp.dma(b_mod[l][:], a[bias].rearrange("(o n) -> o n", o=1).broadcast_to([B, 6 * C]), s_w_mod[l])
                return sp.dma(b_2[l][:], a[b2].rearrange("(o n) -> o n", o=1).broadcast_to([B, C]), s_w_mod[l])

            def modulation(l, loaded):
                done = []
                for j in range(6):
                    bank = psum[3 + j % 5]
                    mm = matmuls([(bank.ap[0:B, 0:C], silu_t[:, i, :], w_mod[l][:, i, C * j:C * j + C]) for i in range(3)],
                                 loaded, silu_t_ok, bank.free)
                    to = order.index(j)
                    r = bank.free = stt(rows[l][:, C * to:C * to + C], bank.ap[0:B, 0:C], 1.0 if j in (1, 4) else 0.0,
                                        b_mod[l][:, C * j:C * j + C], ALU.add, ALU.add, mm, loaded)
                    done.append(r)
                g = tt(dve, rows[l][:, 6 * C:7 * C], rows[l][:, 5 * C:6 * C], b_2[l][:], ALU.mult, done)
                prepared["mod", l] = sp.dma(mod_d[l], rows[l][:], s_mod_rows[l], g)

            mod_loaded = load_modulation(0)

            def load_x(g):
                n = B // X_LOADS
                mark = sp.dma(x_sb[:, TT * n * g:TT * n * (g + 1), :],
                               a["x"][n * g:n * (g + 1)].rearrange("b (t p) c -> p (b t) c", p=P), s_x[g])
                for i in range(TT * n * g, TT * n * (g + 1)):
                    x_marks[i] = mark

            load_x(0)
            raw = sb("raw_qkv", [P, len(WIDE_ROWS), 3 * C])
            for d, src in stacked_moves(raw, "L0_cond_w_qkv", "L0_cond_b_qkv", slice(0, 3 * C), low_chunks=False):
                raw_ok = sp.dma(d, src, s_w)
            mod_1_loaded = load_modulation(1)
            for m, (c0, qk_rows) in enumerate(QK_CHUNKS):
                n = min(qk_rows, C - c0) // HD
                if n > 0:
                    for dst, g in ((qk_gain, "L0_cond_g_q"), (gk_col, "L0_cond_g_k")):
                        gains_loaded = sp.dma(dst[0:n * HD, m:m + 1], a[g].rearrange("(o d) -> o d", o=1).broadcast_to([n, HD]),
                                              s_gain, const_gain)
            prepared["ones"] = sp.dma(ones_d, ones[:], s_ones_out, ones_ok)
            modulation(0, mod_loaded)

            centred = []
            for c0, c1, n in ((0, 2, P), (2, 4, P), (4, 5, WIDE_ROWS[4])):
                means = sb(f"head_means_{c0}", [P, c1 - c0, 2 * HEADS])
                m = means[0:n, :, :]
                qk = raw[0:n, c0:c1, 0:QK].rearrange("p c (h d) -> p c h d", d=HD)
                k = dve.do(lambda q, m=m, qk=qk: q.tensor_reduce(m, qk, AX.X, ALU.add), raw_ok)
                k = dve.do(lambda q, m=m: q.tensor_scalar(m, m, -1.0 / HD, None, ALU.mult), k)
                mb = m.rearrange("p c (h o) -> p c h o", o=1).broadcast_to([n, c1 - c0, 2 * HEADS, HD])
                centred.append(tt(dve, qk, qk, mb, ALU.add, k))
            modulation(1, mod_1_loaded)
            tt(dve, qk_gain[:], qk_gain[:], gk_col[:], ALU.mult, gains_loaded)
            split_ok = split_stacked(raw, w_attn, slice(0, 3 * C), proj_space, centred)
            prepared["attn_weights", 0] = split_ok + load_proj(0, act, split_ok)
            deferred.extend((load_x, g) for g in range(1, X_LOADS))
            for l in range(LAYERS):
                w1, b1, w2 = MLP_WEIGHTS[l]
                for g in range(FC1_LOADS):
                    for d, src in stacked_moves(fc1_d[l][g], w1, b1, slice(group * g, group * (g + 1))):
                        deferred.append((arrange, ("fc1", l), d, src, s_order_fc1[l]))
                for c in range(0, MLP // P, 3):
                    deferred.append((arrange, ("fc2", l), fc2_d[l][:, c:c + 3, :],
                                     a[w2][c * P:(c + 3) * P, :].rearrange("(c p) n -> p c n", p=P), s_order_fc2[l]))
                if l == 0:
                    for d, src in stacked_moves(qkv_d, "L1_cond_W_qkv", "L1_cond_b_qkv", slice(0, 3 * C)):
                        deferred.append((arrange, ("qkv", 1), d, src, s_order_qkv))

        deferred = []

        def arrange(name, dst, src, st):
            prepared[name] = sp.dma(dst, src, st)

        proj_space = w_proj[:].rearrange("p g n -> p (g n)").bitcast(F32R)

        def stacked_moves(dst, w, bias, cols, low_chunks=True):
            w, bias = a[w][:, cols], a[bias].rearrange("(o n) -> o n", o=1)[:, cols]
            low = [(dst[:, 5:7, :], w[0:256, :].rearrange("(i p) n -> p i n", p=P))] if low_chunks else []
            return low + [
                (dst[:, 0:2, :], w[0:256, :].rearrange("(i p) n -> p i n", p=P)),
                (dst[0:32, 2, :], w[256:288, :]), (dst[32:128, 2, :], w[0:96, :]),
                (dst[:, 3, :], w[96:224, :]),
                (dst[0:64, 4, :], w[224:288, :]), (dst[64:96, 4, :], w[256:288, :]),
                (dst[96:98, 4, :], bias.broadcast_to([2, cols.stop - cols.start])),
            ]

        def load_stacked(dst, src, cols, st, *after):
            rows = WIDE_ROWS[4]
            sp.dma(fp(dst[:, 0:4, cols]), src[:, 0:4, :], st, *after)
            sp.dma(fp(dst[0:rows, 4, cols]), src[0:rows, 4, :], st, *after)
            return sp.dma(fp(dst[:, 5:7, cols]), src[:, 5:7, :], st, *after)

        def split_stacked(src, dst, cols, tmp, ready):
            rows = WIDE_ROWS[4]
            mixed, low = dst[0:rows, 4, cols], dst[:, 5:7, cols]
            low_src = src[:, 5:7, cols] if src is dst else src[:, 0:2, cols]
            t = tmp[0:rows, 0:cols.stop - cols.start]
            hk = [copy(act, dst[:, c:c + 2, cols], fp(src[:, c:c + 2, cols]), ready[c // 2]) for c in (0, 2)]
            tk = copy(act, t, fp(src[0:rows, 4, cols]), ready[2])
            lk = tt(dve, low, fp(low_src), fp(dst[:, 0:2, cols]), ALU.subtract, hk[0], ready)
            mk = stt(mixed, fp(t), minus_lo_row[0:rows, :], fp(src[0:rows, 4, cols]), ALU.mult, ALU.add, tk, const_ok, ready)
            return hk + [tk, lk, mk]

        def load_proj(l, queue, *after):
            zero = dve.do(lambda q: q.memset(w_proj[:], 0.0), *after)
            wp, bp = (("L0_cond_w_proj", "L0_cond_b_proj"), ("L1_cond_W_proj", "L1_cond_b_proj"))[l]
            by_head = a[wp].rearrange("(g i d) n -> i d g n", i=PV_HEADS, d=HD)
            for i in range(PV_HEADS):
                queue.dma(w_proj[32 * i:32 * i + HD, :, :], by_head[i], s_w_proj, zero)
            mark = queue.dma(w_proj[HD:HD + 1, 0, :], a[bp].rearrange("(o n) -> o n", o=1), s_w_proj, zero)
            return [mark]

        class Normaliser:

            def __init__(self, sb, ring):
                self.stats = sb("ln_stats", [P, TT, 6])
                self.mv = sb("ln_mean_var", [P, TT, 2])
                self.rstd = sb("ln_rstd", [P, TT])
                self.scaled = sb("ln_scaled", [P, C])
                self.y = [sb(f"ln_modulated{i}", [P, C]) for i in range(2)]
                self.xs = [sb(f"ln_split{i}", [P, XS_COLS], F32R) for i in range(TT)]
                self.xt = [sb(f"ln_transposed{i}", [P, len(WIDE_ROWS), N], F32R) for i in range(ring)]
                self.xt_free = [None] * ring
                self.xs_free = [None] * TT
                self.stats_free = self.mv_free = self.rstd_free = self.scaled_free = None
                self.y_free = [None, None]
                self.mod_read = None
                self.ones_ok = {}

            def place_ones(self, i, *after):
                self.ones_ok[i] = dve.do(lambda q: q.memset(fp(self.xt[i][96:98, 4, :]), 1.0), *after)

            def run(self, b, start, transposes, scale_row, shift_row, mod_ok, take, put):
                hi_cols, lo_cols, dup = slice(0, C), slice(C, 2 * C), slice(2 * C, XS_COLS)
                ring = b % len(self.xt)
                agg = []
                for t in range(TT):
                    xt = x_sb[:, TT * b + t, :]
                    st = dve.do(lambda q, t=t, xt=xt: q.bn_stats(self.stats[:, t, :], xt), x_marks[TT * b + t], self.stats_free)
                    agg.append(dve.do(lambda q, t=t: q.bn_aggr(self.mv[:, t, :], self.stats[:, t, :]), st, self.mv_free))
                    yield start + 1 + t
                self.stats_free = agg
                k = pool.do(lambda q: q.tensor_scalar(self.rstd[:], self.mv[:, :, 1], EPS, None, ALU.add), agg, self.rstd_free)
                rstd_ok = tt(pool, self.rstd[:], self.rstd[:], minus_half[:, 0:TT], ALU.pow, k, const_ok)
                yield start + 3
                done = []

                def modulate(t):
                    u = stt(self.scaled[:], x_sb[:, TT * b + t, :], self.mv[:, t, 0:1], scale_row, ALU.subtract, ALU.mult,
                            agg, mod_ok, self.scaled_free)
                    y = self.scaled_free = stt(self.y[t][:], self.scaled[:], self.rstd[:, t:t + 1], shift_row, ALU.mult, ALU.add,
                                               u, rstd_ok, self.y_free[t])
                    return y

                def high(t, y):
                    return copy(act, self.xs[t][:, hi_cols], self.y[t][:], y, self.xs_free[t])

                def low(t, h):
                    xs = self.xs[t]
                    lo = tt(pool, xs[:, lo_cols], self.y[t][:], fp(xs[:, hi_cols]), ALU.subtract, h, self.xs_free[t])
                    self.y_free[t] = [h, lo]
                    d = copy(pool, xs[:, dup], fp(xs[:, 256:C]), h, self.xs_free[t])
                    done.append([h, lo, d])

                y0 = modulate(0)
                yield start + 4
                y1 = modulate(1)
                self.mv_free = self.rstd_free = self.mod_read = y1
                h0 = high(0, y0)
                yield start + 5
                h1 = high(1, y1)
                low(0, h0)
                yield start + 6
                low(1, h1)
                yield transposes
                evac = []
                pending = None
                for n, pair in enumerate(((0, 1), (2, 3), (4,), None)):
                    if pending:
                        tr, bank, rows, c0, n_c = pending
                        evac.append(copy(act, self.xt[ring][0:rows, c0:c0 + n_c, :],
                                         bank.ap[0:rows, 0:n_c * N].rearrange("p (c n) -> p c n", c=n_c), tr,
                                         self.xt_free[ring], self.ones_ok[ring]))
                        put(bank, evac[-1])
                    if pair is None:
                        break
                    bank = take()
                    rows = 96 if pair == (4,) else P

                    def emit(q, pair=pair, bank=bank, rows=rows):
                        for j, c in enumerate(pair):
                            for t in range(TT):
                                last = q.matmul(bank.ap[0:rows, j * N:j * N + N], self.xs[t][:, c * P:c * P + rows],
                                                ident_wide[:, P - t * P:P - t * P + N], start=(t == 0), stop=(t == TT - 1))
                        return last
                    tr = pe.do(emit, done, bank.free, ident_ok)
                    pending = (tr, bank, rows, pair[0], len(pair))
                    self.xs_free = [tr] * TT
                    yield transposes + 1 + n
                self.ready = (self.xt[ring], evac)


        class MlpStart:

            def __init__(self, l, sb):
                self.l, self.ln = l, Normaliser(sb, 2)
                self.mod = [sb(f"scale_shift{i}", [P, 2 * C]) for i in range(2)]
                self.w1 = sb("w_fc1_stacked", [P, WIDE_CHUNKS, MLP], F32R)
                self.mod_free, self.w1_loaded, self.w1_ok = [None] * 2, [], []

            def front(self, b, start, take, put):
                i, mod, ln = b % 2, self.mod[b % 2], self.ln
                mod_ok = sp.dma(mod[:], mod_d[self.l, b:b + 1, 3 * C:5 * C].broadcast_to([P, 2 * C]), s_mod2[i],
                                self.mod_free[i], prepared["mod", self.l])
                yield start + 2
                yield from ln.run(b, start + 2, start + 10, mod[:, 0:C], mod[:, C:2 * C], mod_ok, take, put)
                self.mod_free[i] = ln.mod_read

            def load_fc1(self):
                g = len(self.w1_loaded)
                self.w1_loaded.append(load_stacked(self.w1, fc1_d[self.l][g], slice(group * g, group * (g + 1)), s_w_fc1[g],
                                                   prepared["fc1", self.l]))

            def split_fc1(self):
                g = len(self.w1_ok)
                scratch_w = self.ln.xt[1][:].rearrange("p c n -> p (c n)")[:, group * g:group * (g + 1)]
                self.w1_ok.append(split_stacked(self.w1, self.w1, slice(group * g, group * (g + 1)), scratch_w, [self.w1_loaded[g]] * 3))
                self.ln.xt_free[1] = list(self.w1_ok)

        mlp_start = []

        def attention(l):
            def run(sb, rest_before):
                with ExitStack() as early:
                    start = MlpStart(l, lambda n, shape, dt=F32: sb_in(early, f"mlp{l}_{n}", shape, dt))
                mlp_start.append(start)
                banks = Banks(psum[8 - PSUM_RING:])
                take, put = banks.take, banks.put

                ln = Normaliser(sb, 1)
                ln.place_ones(0)
                mod = sb("scale_shift", [P, 2 * C])
                parts = [sb(f"qk_parts{i}", [P, 3, N], BF16) for i in range(PARTS_RING)]
                rest = [sb(f"qk_rest{i}", [P, N]) for i in range(2)]
                if l == 0:
                    z_sb = [sb(f"qk_centred{i}", [P, N]) for i in range(Z_RING)]
                    sq_sb = [sb(f"qk_squares{i}", [P, N]) for i in range(2)]
                    rstd_sb = [sb(f"qk_rstd{i}", [P, N]) for i in range(2)]
                else:
                    sb("room_of_the_head_norm", [P, (Z_RING + 4) * N])
                maxes = [sb(f"maxima{i}", [P, HEADS, TT]) for i in range(2)]
                q_st, k_st = {}, {}
                for i in sorted(range(STACK_RING), key=lambda i: i == (B - 1) % STACK_RING):
                    q_st[i] = sb(f"q_stack{i}", [P, HEADS, N], BF16)
                    k_st[i] = sb(f"k_stack{i}", [P, HEADS, N], BF16)
                v_sb = [sb(f"v{i}", [P, TT, HEADS, VW]) for i in range(V_RING)]
                probs = [sb(f"probs{i}", [P, TT * N]) for i in range(P_RING)]
                neg_hi = sb("neg_max_hi", [HEADS * TT, P], BF16)
                neg_lo = sb("neg_max_lo", [HEADS * TT, P], BF16)
                gate = sb("gate", [P, C])
                o_t = [sb(f"o_transposed{i}", [P, GROUPS * N]) for i in range(2)]
                recip_b = sb("reciprocals", [P, GROUPS * N])
                sums = sb("row_sums", [P, PV_HEADS * GROUPS * N // P])
                recip = sb("row_reciprocals", [P, PV_HEADS * GROUPS * N // P])
                gated = sb("gated", [P, C])

                w_ok = prepared["attn_weights", l]
                k_ones, v_one = [], []
                pv = psum[4]

                if l == 0:
                    act.queue.append(lambda q: q.preload_act_table_set("natural_log_exp_and_others"))
                parts_free = [None] * PARTS_RING
                rest_free, z_free = [None, None], [None] * Z_RING
                part_marks = {}
                stack_ok, v_ok = {}, {}
                scratch_free = [None, None]
                last_scores = {}
                max_ok, max_t_ok, exp_ok, pv_done, neg_ok = {}, {}, {}, {}, {}
                smax_free, st_free = [None, None], [None, None]
                probs_free = [None] * P_RING
                sq_free, rstd_free = [None, None], [None, None]
                state = {"gate_free": None, "neg": None, "recip": None, "recip_b": None, "gated": None}
                o_free = [None, None]
                v_free = [None] * V_RING

                def load_mod(b):
                    return sp.dma(mod[:], mod_d[l, b:b + 1, 0:2 * C].broadcast_to([P, 2 * C]), s_mod, ln.mod_read,
                                  prepared["mod", l])

                chunks_done = [0]

                def qk_chunk(b, m, xt, xt_ok):
                    c0, rows = QK_CHUNKS[m]
                    slot = HEADS * b + CHUNK_SLOTS[m]
                    bank = take()
                    mm = matmuls(wide_steps(bank.ap[0:rows, 0:N], w_attn, xt, (c0, c0 + rows), (0, N), True),
                                 xt_ok, w_ok, bank.free)
                    n = chunks_done[0]
                    chunks_done[0] += 1
                    i, pi, zi = n % 2, n % PARTS_RING, n % Z_RING
                    a_part, b_part, c_part = (parts[pi][0:rows, j, :] for j in range(3))
                    r = rest[i][0:rows, :]
                    yield slot + 1
                    if l == 1:
                        ak = copy(act, a_part, bank.ap[0:rows, 0:N], mm, parts_free[pi])
                        yield slot + 2
                        rk = put(bank, tt(dve, r, bank.ap[0:rows, 0:N], a_part, ALU.subtract, ak, rest_free[i]))
                        yield slot + 3
                        bk = copy(act, b_part, r, rk, parts_free[pi])
                        yield slot + 4
                    else:
                        z, sq, qk_rstd = z_sb[zi][0:rows, :], sq_sb[i][0:rows, :], rstd_sb[i][0:rows, :]
                        zk = put(bank, copy(act, z, bank.ap[0:rows, 0:N], mm, z_free[zi]))
                        sk = func(sq, z, ACT.Square, zk, sq_free[i])
                        yield slot + 2
                        bank = take()
                        vk = sq_free[i] = pe.do(lambda q: q.matmul(bank.ap[0:rows, 0:N], head_ones[0:rows, 0:rows],
                                                                   sq, start=True, stop=True),
                                                sk, bank.free, head_ones_ok)
                        yield slot + 3
                        lk = put(bank, func(qk_rstd, bank.ap[0:rows, 0:N], ACT.Ln, vk, rstd_free[i], const_ok,
                                            bias=eps_col[0:rows, :], scale=1.0 / HD))
                        ek = func(qk_rstd, qk_rstd, ACT.Exp, lk, scale=-0.5)
                        yield slot + 4
                        yk = rstd_free[i] = stt(z, z, qk_gain[0:rows, m:m + 1], qk_rstd, ALU.mult, ALU.mult, ek, zk)
                        yield slot + 5
                        ak = copy(act, a_part, z, yk, parts_free[pi])
                        yield slot + 6
                        rk = z_free[zi] = tt(dve, r, z, a_part, ALU.subtract, ak, rest_free[i])
                        bk = copy(dve, b_part, r, rk, parts_free[pi])
                        yield slot + 7
                    ck = rest_free[i] = tt(pool, c_part, r, b_part, ALU.subtract, bk)
                    dst = parts_d[b % 2][:, c0:c0 + rows, :].rearrange("j r n -> r j n")
                    part_marks[b, m] = parts_free[pi] = sp.dma(dst, parts[pi][0:rows, :, :], s_parts[m], ck, scratch_free[b % 2])

                def load_stacks(b):
                    ring, d = b % STACK_RING, parts_d[b % 2]
                    after = [part_marks[b, m] for m in range(len(QK_CHUNKS))] + [last_scores.get(b - STACK_RING), k_ones[-1]]
                    for j, (qp, kp) in enumerate(((0, 0), (0, 1), (0, 2), (1, 0), (1, 1), (2, 0))):
                        for st, p, c0 in ((q_st, qp, 0), (k_st, kp, C)):
                            mark = sp.dma(st[ring][HD * j:HD * j + HD, :, :],
                                          d[p, c0:c0 + C, :].rearrange("(h r) n -> r h n", r=HD), s_stack[ring], after)
                    stack_ok[b] = scratch_free[b % 2] = mark


                def value_tile(b, t, xt, xt_ok):
                    bank = take()
                    mm = matmuls(wide_steps(bank.ap[:, 0:C], w_attn, xt, (QK, 3 * C), (t * P, t * P + P), False),
                                 xt_ok, w_ok, bank.free)
                    ln.xt_free = [mm]
                    yield HEADS * b + VALUE_SLOTS[t] + 1
                    vk = copy(dve, v_sb[b % V_RING][:, t, :, 0:HD], bank.ap[:, 0:C].rearrange("p (h d) -> p h d", d=HD),
                              mm, v_free[b % V_RING], v_one)
                    v_ok.setdefault(b, []).append(put(bank, vk))

                def front(b):
                    mod_ok = load_mod(b)
                    start = HEADS * b + FRONT_START
                    yield start + 3
                    yield from ln.run(b, start + 3, start + 18, mod[:, 0:C], mod[:, C:2 * C], mod_ok, take, put)
                    xt, xt_ok = ln.ready
                    for m, slot in enumerate(CHUNK_SLOTS):
                        yield HEADS * b + slot
                        yield qk_chunk(b, m, xt, xt_ok)
                    for t, slot in enumerate(VALUE_SLOTS):
                        yield HEADS * b + slot
                        yield value_tile(b, t, xt, xt_ok)
                    yield HEADS * b + STACKS_SLOT
                    load_stacks(b)

                def place_maxima(b):
                    slot = HEADS * b - MAX_LEAD + HEADS + 1
                    yield slot + 1
                    bank = take()
                    rows = HEADS * TT
                    tr = max_t_ok[b] = pe.do(
                        lambda q: q.transpose(bank.ap[0:rows, 0:P], maxes[b % 2][:].rearrange("p h t -> p (h t)"), ident),
                        max_ok[b, HEADS - 1], bank.free, ident_ok)
                    yield slot + 2
                    hk = dve.do(lambda q: q.tensor_scalar(neg_hi[:], bank.ap[0:rows, 0:P], -1.0, None, ALU.mult), tr, state["neg"])
                    lk = put(bank, stt(neg_lo[:], bank.ap[0:rows, 0:P], -1.0, neg_hi[:], ALU.mult, ALU.subtract, hk))
                    yield slot + 3
                    for src, row in ((neg_hi, STACK), (neg_lo, STACK + 1)):
                        dst = q_st[b % STACK_RING][row:row + 1, :, :].rearrange("o h (t n) -> o (h t) n", t=TT)
                        neg_ok[b] = state["neg"] = sp.dma(dst, src[:], s_max, lk, last_scores.get(b - STACK_RING))

                def max_scores(b, h):
                    ring, i = b % STACK_RING, h % 2
                    bank = psum[i]
                    qs, ks = q_st[ring], k_st[ring]

                    def emit(q):
                        for t in range(TT):
                            last = q.matmul(bank.ap[:, t * N:t * N + N], qs[0:STACK, h, t * P:t * P + P], ks[0:STACK, h, :],
                                            start=True, stop=True)
                        return last
                    return pe.do(emit, stack_ok[b], smax_free[i])

                def reduce_max(b, h, mm):
                    i = h % 2
                    max_ok[b, h] = smax_free[i] = dve.do(
                        lambda q: q.tensor_reduce(maxes[b % 2][:, h, :], psum[i].ap[:].rearrange("p (t n) -> p t n", t=TT), AX.X, ALU.max),
                        mm, max_t_ok.get(b - 2))

                def shifted_scores(b, h):
                    ring, i = b % STACK_RING, h % 2
                    bank = psum[2 + i]
                    qs, ks = q_st[ring], k_st[ring]

                    def emit(q):
                        for t in range(TT):
                            last = q.matmul(bank.ap[:, t * N:t * N + N], ks[0:STACK + 2, h, t * P:t * P + P],
                                            qs[0:STACK + 2, h, :], start=True, stop=True)
                        return last
                    mm = pe.do(emit, stack_ok[b], neg_ok[b], st_free[i])
                    last_scores[b] = mm
                    return mm

                def exponentials(b, h, mm):
                    i = h % 2
                    r = (b * HEADS + h) % P_RING
                    exp_ok[b, h] = st_free[i] = func(probs[r][:], psum[2 + i].ap[:], ACT.Exp, mm, probs_free[r], scale=SCORE_SCALE)

                def weigh_values(b, g):
                    def emit(q):
                        for t in range(TT):
                            for i in range(PV_HEADS):
                                h = g * PV_HEADS + i
                                r = (b * HEADS + h) % P_RING
                                last = q.matmul(pv.ap[32 * i:32 * i + VW, 0:N], v_sb[b % V_RING][:, t, h, :],
                                                probs[r][:, t * N:t * N + N], start=(t == 0), stop=(t == TT - 1))
                        return last
                    mm = pe.do(emit, v_ok[b], [exp_ok[b, g * PV_HEADS + i] for i in range(PV_HEADS)], pv.free)
                    for i in range(PV_HEADS):
                        probs_free[(b * HEADS + g * PV_HEADS + i) % P_RING] = mm
                    v_free[b % V_RING] = mm
                    return mm

                def values(b, g, slot):
                    mm = weigh_values(b, g)
                    yield slot + 1
                    pv_done[b, g] = pv.free = copy(act, o_t[b % 2][:, g * N:g * N + N], pv.ap[:, 0:N], mm, o_free[b % 2])

                    if g == GROUPS - 1:
                        yield back(b)

                def back(b):
                    first = HEADS * b + HEADS + 2
                    o = o_t[b % 2]
                    yield first + 1
                    k = sp.dma(sums[:], o[HD:HD + 97:32, :].rearrange("i (q n) -> i q n", n=sums.shape[1]), s_sums,
                               pv_done[b, GROUPS - 1], state["recip"])
                    yield first + 4
                    rk = dve.do(lambda q: q.reciprocal(recip[:], sums[:]), k, state["recip"])
                    yield first + 5
                    state["recip"] = k = sp.dma(recip_d.rearrange("i (q n) -> (i q) n", n=sums.shape[1]), recip[:], s_recip, rk,
                                                state["recip_b"])
                    yield first + 7
                    bk = sp.dma(recip_b[:], recip_d.rearrange("i (o n) -> i o n", o=1).broadcast_to([PV_HEADS, 32, GROUPS * N]),
                                s_recip_in, k, state["recip_b"])
                    gate_ok = sp.dma(gate[:], mod_d[l, b:b + 1, 2 * C:3 * C].broadcast_to([P, C]), s_gate, state["gate_free"],
                                     prepared["mod", l])
                    yield first + 11
                    half = GROUPS * N // 2
                    nk = []
                    for j, engine in enumerate((dve, pool)):
                        cols = slice(half * j, half * j + half)
                        nk.append(tt(engine, o[:, cols], o[:, cols], recip_b[:, cols], ALU.mult, bk))
                    state["recip_b"] = nk
                    for t, (slot, second) in enumerate(PROJ_SLOTS):
                        yield HEADS * b + slot
                        bank = take()

                        def project(groups, t=t, bank=bank):
                            def emit(q):
                                for g in groups:
                                    last = q.matmul(bank.ap[:, 0:C], o[:, g * N + t * P:g * N + t * P + P], w_proj[:, g, :],
                                                    start=(g == 0), stop=(g == GROUPS - 1))
                                return last
                            return pe.do(emit, nk, w_ok, bank.free)

                        project(range(GROUPS // 2))
                        yield HEADS * b + second
                        mm = project(range(GROUPS // 2, GROUPS))
                        yield gate_and_add(b, t, bank, mm, HEADS * b + second, gate_ok)
                    o_free[b % 2] = mm

                def gate_and_add(b, t, bank, mm, slot, gate_ok):
                    yield slot + 1
                    gk = state["gate_free"] = put(bank, tt(dve, gated[:], bank.ap[:, 0:C], gate[:], ALU.mult, mm, gate_ok,
                                                           state["gated"]))
                    yield slot + 2
                    xt = x_sb[:, TT * b + t, :]
                    x_marks[TT * b + t] = state["gated"] = tt(pool, xt, xt, gated[:], ALU.add, gk)

                agenda = Agenda(FRONT_START)
                maxima = exps = None
                for T in range(FRONT_START, HEADS * B + 3):
                    b, h = divmod(T, HEADS)
                    if rest_before:
                        rest_before = rest_before()
                    if T == FRONT_START + REST_SLOTS:
                        assert not rest_before
                        meet()
                        for t in k_st.values():
                            k_ones.append(sp.dma(t[STACK:STACK + 2, :, :], ones_d, s_ones, prepared["ones"]))
                        for t in v_sb:
                            dve.do(lambda q, t=t: q.memset(t[:, :, :, HD:HD + 1], 1.0))
                            v_one.append(dve.do(lambda q, t=t: q.memset(t[:, :, :, HD + 1:VW], 0.0)))
                        pv.free = dve.do(lambda q: q.memset(pv.ap[:, 0:N], 0.0))
                    to_end = T - HEADS * B
                    if to_end == LEFT_SLOT:
                        left = all_so_far()
                    if to_end == MLP_FRONT_SLOT:
                        for e in engines:
                            e.wait(left)
                        start.ln.place_ones(0)
                        agenda.start(start.front(0, T, take, put), last=True)
                    if to_end in FC1_LOAD_SLOTS:
                        if to_end == FC1_LOAD_SLOTS[0]:
                            meet(sp)
                        start.load_fc1()
                    if to_end in FC1_SPLIT_SLOTS:
                        start.split_fc1()
                    if deferred and T >= DEFERRED_START and T % HEADS in DEFERRED_SLOTS:
                        call, *args = deferred.pop(0)
                        call(*args)
                    if exps:
                        exponentials(*exps)
                    if maxima:
                        reduce_max(*maxima)
                        if maxima[1] == HEADS - 1:
                            agenda.start(place_maxima(maxima[0]))
                    mb, mh = divmod(T + MAX_LEAD, HEADS)
                    maxima = (mb, mh, max_scores(mb, mh)) if 0 <= mb < B else None
                    exps = (b, h, shifted_scores(b, h)) if 0 <= b < B else None
                    fb, fh = divmod(T - FRONT_START, HEADS)
                    if fh == 0 and fb < B:
                        agenda.start(front(fb), last=True)
                    agenda.run(T)
                    vb, vh = divmod(T - 2, HEADS)
                    if 0 <= vb < B and vh % PV_HEADS == PV_HEADS - 1:
                        agenda.start(values(vb, vh // PV_HEADS, T))
                meet()
                return rest_of(agenda, HEADS * B + 3)
            return run

        CHUNKS = MLP // P
        SLOTS = CHUNKS + 6

        def mlp(l):
            def run(sb, rest_before):
                banks = Banks(psum[:8 - PSUM_RING])
                take, put = banks.take, banks.put

                MlpStart(l, lambda n, shape, dt=F32: sb(f"place_of_{n}", shape, dt))
                start = mlp_start[l]
                w1, w1_ok, ln = start.w1, start.w1_ok, start.ln
                w2 = {part: sb(f"w_fc2_{part}", [P, CHUNKS, C], F32R) for part in ("hi", "lo")}
                gate = [sb(f"gate_and_gated_bias{i}", [P, 2 * C]) for i in range(2)]
                hidden = [sb(f"hidden{i}", [P, N]) for i in range(3)]
                gated = [sb(f"gated{i}", [P, C]) for i in range(TT)]
                h_hi, h_lo = [], []
                for i in range(2):
                    h_hi.append(sb(f"hidden_hi{i}", [P, CHUNKS, N], F32R))
                    h_lo.append(sb(f"hidden_lo{i}", [P, CHUNKS, N], F32R))
                gate_free, h_free, gated_free = [None] * 2, [None] * 2, [None] * TT
                hidden_free = [None] * 3
                chunks_done = [0]
                w2_ok, h_split = [], {}

                def fc1(b):
                    i, first = b % 2, SLOTS * b
                    xt, xt_ok = ln.ready
                    h_split[b] = []
                    for m in range(CHUNKS):
                        yield first + m
                        bank = take()
                        mm = matmuls(wide_steps(bank.ap[:, 0:N], w1, xt, (m * P, m * P + P), (0, N), True), xt_ok,
                                     w1_ok[m * P // group], bank.free)
                        yield activate(b, m, bank, mm, first + m)
                    ln.xt_free[i] = mm

                def activate(b, m, bank, mm, slot):
                    i, r = b % 2, chunks_done[0] % 3
                    chunks_done[0] += 1
                    yield slot + 1
                    gk = put(bank, func(hidden[r][:], bank.ap[:, 0:N], ACT.Gelu_apprx_tanh, mm, hidden_free[r]))
                    yield slot + 2
                    after = [h_free[i], h_ready]
                    hk = copy(dve, h_hi[i][:, m, :], hidden[r][:], gk, after)
                    lk = hidden_free[r] = tt(dve, h_lo[i][:, m, :], hidden[r][:], fp(h_hi[i][:, m, :]), ALU.subtract, hk, after)
                    h_split[b] += [hk, lk]

                def fc2(b):
                    i, first = b % 2, SLOTS * b + SLOTS + CHUNKS
                    yield first - 5
                    gate_ok[b] = sp.dma(gate[i][:], mod_d[l, b:b + 1, 5 * C:7 * C].broadcast_to([P, 2 * C]), s_gate2[i],
                                        gate_free[i], prepared["mod", l])
                    yield first
                    for t in range(TT):
                        bank = take()
                        cols = slice(t * P, t * P + P)
                        for third in range(3):
                            yield first + 3 * t + third

                            def emit(q, bank=bank, cols=cols, third=third):
                                for c in range(3 * third, 3 * third + 3):
                                    for x, w in ((h_hi, "hi"), (h_hi, "lo"), (h_lo, "hi")):
                                        last = q.matmul(bank.ap[:, 0:C], x[i][:, c, cols], w2[w][:, c, :],
                                                        start=(c == 0 and x is h_hi and w == "hi"),
                                                        stop=(c == CHUNKS - 1 and x is h_lo))
                                return last
                            mm = pe.do(emit, h_split[b], w2_ok, bank.free)
                        yield gate_and_add(b, t, bank, mm, first + 3 * t + 2)
                    h_free[i] = mm

                def gate_and_add(b, t, bank, mm, slot):
                    i = b % 2
                    yield slot + 1
                    gk = put(bank, tt(dve, gated[t][:], bank.ap[:, 0:C], gate[i][:, 0:C], ALU.mult, mm, gate_ok[b], gated_free[t]))
                    yield slot + 2
                    xt = x_sb[:, TT * b + t, :]
                    k = gated_free[t] = tt(pool, xt, xt, gated[t][:], ALU.add, gk)
                    k = x_marks[TT * b + t] = gate_free[i] = tt(pool, xt, xt, gate[i][:, C:2 * C], ALU.add, k)
                    if t == TT - 1 and l == LAYERS - 1:
                        yield slot + 4
                        sp.dma(out[b].rearrange("(t p) c -> p t c", p=P), x_sb[:, TT * b:TT * b + TT, :], s_out, k)

                gate_ok = {}
                h_ready = None
                agenda = Agenda(MLP_FIRST_SLOT)
                last = l == LAYERS - 1
                for T in range(MLP_FIRST_SLOT, SLOTS * (B + 1) + 6 if last else SLOTS * B + 4):
                    b, s = divmod(T, SLOTS)
                    if rest_before:
                        rest_before = rest_before()
                        if not rest_before:
                            h_ready = [(e.sem, e.count) for e in (pe, dve, pool)] + [(s_gate.sem, s_gate.count)]
                            banks.idle += psum[8 - PSUM_RING:]
                    if T == MLP_FIRST_SLOT:
                        start.split_fc1()
                        ln.place_ones(1, w1_ok)
                    if T == FC2_LOAD_SLOT:
                        w2_raw = sp.dma(fp(w2["lo"][:]), fc2_d[l], s_w_fc2, prepared["fc2", l])
                    if s == 0:
                        if b + 1 < B:
                            agenda.start(start.front(b + 1, T, take, put))
                        if 0 <= b < B:
                            agenda.start(fc1(b))
                            agenda.start(fc2(b))
                        if b == 2 and not last:
                            raw_ok = load_stacked(w_attn, qkv_d, slice(0, 3 * C), s_w, prepared["qkv", 1])
                        if b == 4 and not last:
                            split_ok = split_stacked(w_attn, w_attn, slice(0, 3 * C), proj_space, [raw_ok] * 3)
                            prepared["attn_weights", l + 1] = split_ok + load_proj(l + 1, sp, split_ok)
                    if T == FC2_SPLIT_SLOT:
                        w2_ok.append(copy(act, w2["hi"][:], fp(w2["lo"][:]), w2_raw))
                        w2_ok.append(tt(dve, w2["lo"][:], fp(w2["lo"][:]), fp(w2["hi"][:]), ALU.subtract, w2_ok[0]))
                    agenda.run(T)
                meet()
                if last:
                    return None
                assert len(banks.idle) == 8
                banks.idle = [bk for bk in banks.idle if bk in psum[:8 - PSUM_RING]]
                return rest_of(agenda, SLOTS * B + 4)
            return run

        phase("prep", prepare)
        meet()
        rest = None
        for l in range(LAYERS):
            rest = phase(f"attn{l}", attention(l), rest)
            rest = phase(f"mlp{l}", mlp(l), rest)

        block = outer.enter_context(nc.Block())
        block.tensor(pe.play)
        block.scalar(act.play)
        block.vector(dve.play)
        block.gpsimd(pool.play)
        block.sync(sp.play)


_INS = ['x', 'cond_1152', 'L0_cond_w_mod', 'L0_cond_b_mod', 'L0_cond_w_qkv', 'L0_cond_b_qkv', 'L0_cond_g_q', 'L0_cond_g_k',
        'L0_cond_w_proj', 'L0_cond_b_proj', 'L0_cond_w1', 'L0_cond_b1', 'L0_cond_w2', 'L0_cond_b2',
        'L1_cond_W_qkv', 'L1_cond_b_qkv', 'L1_cond_W_proj', 'L1_cond_b_proj', 'L1_cond_W_fc1', 'L1_cond_b_fc1',
        'L1_cond_W_fc2', 'L1_cond_b_fc2', 'L1_cond_W_ada', 'L1_cond_b_ada']


def kernel(**inputs):
    import numpy as _np
    import concourse.bacc as _bacc
    from concourse import mybir as _mybir
    from concourse.bass_utils import run_bass_kernel_spmd as _run

    nc = _bacc.Bacc("TRN2", target_bir_lowering=False, num_devices=1, dynamic_dma_scratch_size=64)
    arrays, aps = {}, {}
    for name in _INS:
        v = _np.ascontiguousarray(inputs[name])
        arrays[f"in_{name}_dram"] = v
        aps[name] = nc.dram_tensor(f"in_{name}_dram", v.shape, _mybir.dt.from_np(v.dtype), kind="ExternalInput").ap()
    out = nc.dram_tensor("out_0_dram", (B, N, C), F32, kind="ExternalOutput").ap()
    build(nc, aps, out)
    r = _run(nc, [arrays], core_ids=[0])
    return r.results[0]["out_0_dram"]
```
